# Optimizing a Trainium2 kernel written in Bass

```python
import numpy as np
import jax
import jax.numpy as jnp

def _softmax(x, axis=-1):
    return jax.nn.softmax(x, axis=axis)

def _gelu(x):
    return jax.nn.gelu(x, approximate=True)

def _silu(x):
    return jax.nn.silu(x)

def _sigmoid(x):
    return jax.nn.sigmoid(x)

def _layernorm(x, axis=-1, eps=1e-05):
    m = jnp.mean(x, axis=axis, keepdims=True)
    v = jnp.var(x, axis=axis, keepdims=True)
    return (x - m) / jnp.sqrt(v + eps)

def _scatter_add(tgt, idx, src, axis=0):
    return tgt.at[idx].add(src)

def _segment_sum(src, seg, n):
    return jax.ops.segment_sum(src, seg, n)
kernel_name = 'mk_prb_d1_jaxref_r4_b32457'

def setup_inputs(seed: int=0):
    np.random.seed(seed)
    _w = jnp.asarray

    def _L0_attn_setup():
        import jax, jax.numpy as jnp
        import numpy as np
        NUM_HEADS = 16
        GROUP_SIZE = 4
        DIM = 256
        HEAD_DIM = DIM // NUM_HEADS
        NUM_GROUPS = max(1, NUM_HEADS // GROUP_SIZE)
        SCALE = HEAD_DIM ** (-0.5)
        key = jax.random.key(seed)
        k1, k2, k3, k4, k5 = jax.random.split(key, 5)
        B, T = (1, 1024)
        x = jax.random.normal(k1, (B, T, DIM), dtype=jnp.float32)
        Wq = jax.random.normal(k2, (DIM, NUM_HEADS * HEAD_DIM), dtype=jnp.float32) * DIM ** (-0.5)
        Wk = jax.random.normal(k3, (DIM, NUM_GROUPS * HEAD_DIM), dtype=jnp.float32) * DIM ** (-0.5)
        Wv = jax.random.normal(k4, (DIM, NUM_GROUPS * HEAD_DIM), dtype=jnp.float32) * DIM ** (-0.5)
        Wo = jax.random.normal(k5, (NUM_HEADS * HEAD_DIM, DIM), dtype=jnp.float32) * DIM ** (-0.5)
        return {'x': x, 'Wq': Wq, 'Wk': Wk, 'Wv': Wv, 'Wo': Wo}
    _L0_attn_in = _L0_attn_setup()

    def _L0_ffn_setup():
        import jax, jax.numpy as jnp
        import numpy as np
        from jax import lax
        TOP_K = 4
        N_GROUP = 4
        TOPK_GROUP = 2
        ROUTED_SCALE = 2.5
        NEG_INF = -1000000000.0

        def _route(xf, router_weight, router_bias):
            T = xf.shape[0]
            E = router_weight.shape[0]
            logits = xf @ router_weight.T
            scores = jax.nn.sigmoid(logits)
            s_choice = scores + router_bias
            per_group = E // N_GROUP
            sg = s_choice.reshape(T, N_GROUP, per_group)
            group_scores = lax.top_k(sg, 2)[0].sum(-1)
            _, gidx = lax.top_k(group_scores, TOPK_GROUP)
            gmask = jnp.zeros((T, N_GROUP), dtype=bool).at[jnp.arange(T)[:, None], gidx].set(True)
            masked = jnp.where(gmask[:, :, None], sg, NEG_INF).reshape(T, E)
            _, topk_idx = lax.top_k(masked, TOP_K)
            w = jnp.take_along_axis(scores, topk_idx, axis=1)
            w = w / (w.sum(-1, keepdims=True) + 1e-20) * ROUTED_SCALE
            combine = jnp.zeros((T, E), dtype=xf.dtype).at[jnp.arange(T)[:, None], topk_idx].add(w)
            return combine
        key = jax.random.key(seed)
        ks = jax.random.split(key, 6)
        B, S, H, I, E = (2, 512, 256, 128, 16)
        x = jax.random.normal(ks[0], (B, S, H), dtype=jnp.float32)
        router_weight = jax.random.normal(ks[1], (E, H), dtype=jnp.float32) * 0.02
        router_bias = jnp.zeros((E,), dtype=jnp.float32)
        w_gate = jax.random.normal(ks[2], (E, I, H), dtype=jnp.float32) * 0.02
        w_up = jax.random.normal(ks[3], (E, I, H), dtype=jnp.float32) * 0.02
        w_down = jax.random.normal(ks[4], (E, H, I), dtype=jnp.float32) * 0.02
        return {'x': x, 'router_weight': router_weight, 'router_bias': router_bias, 'w_gate': w_gate, 'w_up': w_up, 'w_down': w_down}
    _L0_ffn_in = _L0_ffn_setup()
    _d = {'L0_attn_x': _L0_attn_in['x'], 'L0_attn_Wq': _L0_attn_in['Wq'], 'L0_attn_Wk': _L0_attn_in['Wk'], 'L0_attn_Wv': _L0_attn_in['Wv'], 'L0_attn_Wo': _L0_attn_in['Wo'], 'L0_ffn_router_weight': _L0_ffn_in['router_weight'], 'L0_ffn_router_bias': _L0_ffn_in['router_bias'], 'L0_ffn_w_gate': _L0_ffn_in['w_gate'], 'L0_ffn_w_up': _L0_ffn_in['w_up'], 'L0_ffn_w_down': _L0_ffn_in['w_down']}
    _x0 = _d['L0_attn_x']
    _d['L0_attn_x'] = jax.random.normal(jax.random.fold_in(jax.random.key(seed), 1), (4, 1024, 256), dtype=_x0.dtype)
    del _x0
    return _d

def reference(L0_attn_x, L0_attn_Wq, L0_attn_Wk, L0_attn_Wv, L0_attn_Wo, L0_ffn_router_weight, L0_ffn_router_bias, L0_ffn_w_gate, L0_ffn_w_up, L0_ffn_w_down):

    def _L0_attn_ref(x, Wq, Wk, Wv, Wo):
        import jax, jax.numpy as jnp
        import numpy as np
        NUM_HEADS = 16
        GROUP_SIZE = 4
        DIM = 256
        HEAD_DIM = DIM // NUM_HEADS
        NUM_GROUPS = max(1, NUM_HEADS // GROUP_SIZE)
        SCALE = HEAD_DIM ** (-0.5)
        B, T, C = x.shape
        rep = NUM_HEADS // NUM_GROUPS
        q = (x @ Wq).reshape(B, T, NUM_HEADS, HEAD_DIM)
        k = (x @ Wk).reshape(B, T, NUM_GROUPS, HEAD_DIM)
        v = (x @ Wv).reshape(B, T, NUM_GROUPS, HEAD_DIM)
        k = jnp.repeat(k, rep, axis=2)
        v = jnp.repeat(v, rep, axis=2)
        scores = jnp.einsum('bqhd,bkhd->bhqk', q, k) * SCALE
        weights = jax.nn.softmax(scores, axis=-1)
        out = jnp.einsum('bhqk,bkhd->bqhd', weights, v)
        out = out.reshape(B, T, NUM_HEADS * HEAD_DIM)
        return out @ Wo

    def _L0_ffn_ref(x, router_weight, router_bias, w_gate, w_up, w_down):
        import jax, jax.numpy as jnp
        import numpy as np
        from jax import lax
        TOP_K = 4
        N_GROUP = 4
        TOPK_GROUP = 2
        ROUTED_SCALE = 2.5
        NEG_INF = -1000000000.0

        def _route(xf, router_weight, router_bias):
            T = xf.shape[0]
            E = router_weight.shape[0]
            logits = xf @ router_weight.T
            scores = jax.nn.sigmoid(logits)
            s_choice = scores + router_bias
            per_group = E // N_GROUP
            sg = s_choice.reshape(T, N_GROUP, per_group)
            group_scores = lax.top_k(sg, 2)[0].sum(-1)
            _, gidx = lax.top_k(group_scores, TOPK_GROUP)
            gmask = jnp.zeros((T, N_GROUP), dtype=bool).at[jnp.arange(T)[:, None], gidx].set(True)
            masked = jnp.where(gmask[:, :, None], sg, NEG_INF).reshape(T, E)
            _, topk_idx = lax.top_k(masked, TOP_K)
            w = jnp.take_along_axis(scores, topk_idx, axis=1)
            w = w / (w.sum(-1, keepdims=True) + 1e-20) * ROUTED_SCALE
            combine = jnp.zeros((T, E), dtype=xf.dtype).at[jnp.arange(T)[:, None], topk_idx].add(w)
            return combine
        B, S, H = x.shape
        E = w_gate.shape[0]
        xf = x.reshape(-1, H)
        combine = _route(xf, router_weight, router_bias)
        out = jnp.zeros_like(xf)
        for e in range(E):
            g = xf @ w_gate[e].T
            u = xf @ w_up[e].T
            y_e = jax.nn.silu(g) * u @ w_down[e].T
            out = out + combine[:, e:e + 1] * y_e
        return out.reshape(B, S, H)
    x = L0_attn_x
    xn = _layernorm(x, axis=-1)
    x = x + _L0_attn_ref(xn, L0_attn_Wq, L0_attn_Wk, L0_attn_Wv, L0_attn_Wo) + _L0_ffn_ref(xn, L0_ffn_router_weight, L0_ffn_router_bias, L0_ffn_w_gate, L0_ffn_w_up, L0_ffn_w_down)
    return x

_drawn_inputs = setup_inputs


def setup_inputs(seed=0):
    import zlib

    import numpy as np

    out = dict(_drawn_inputs(seed))
    spreads = {'L0_ffn_router_bias': (0.0, 0.61)}
    factors = {'L0_ffn_router_weight': 4.779,
     'L0_ffn_w_gate': 3.821,
     'L0_ffn_w_up': 3.777,
     'L0_ffn_w_down': 3.772}
    for name, (base, spread) in spreads.items():
        noise = np.random.default_rng([zlib.crc32(name.encode()), seed]).standard_normal(out[name].shape)
        drawn = base * np.exp(spread * noise) if base else spread * noise
        out[name] = jnp.asarray(drawn.astype(out[name].dtype))
    for name, factor in factors.items():
        out[name] = (out[name] * factor).astype(out[name].dtype)
    return out
```

```python
from contextlib import ExitStack

import concourse.bass as bass
from concourse import mybir

F32 = mybir.dt.float32
F32R = mybir.dt.float32r
BF16 = mybir.dt.bfloat16
ALU = mybir.AluOpType
ACT = mybir.ActivationFunctionType
AX_X = mybir.AxisListType.X

P = 128
BANK = 512
LN_EPS = 1e-5
ROUTED_SCALE = 2.5
NEG_INF = -1.0e9
Q_PARTS = (0, 0, 1, 1, 0, 2)
K_PARTS = (0, 1, 0, 1, 2, 0)


def build_layer(nc, x, wq, wk, wv, wo, wr, bias, wg, wu, wd, out):
    NB, SEQ, D = x.shape
    T = NB * SEQ
    NT = T // P
    KC = D // P
    KV = wk.shape[1]
    HD = 16
    NH = D // HD
    NG = KV // HD
    REP = NH // NG
    E, _, I = wg.shape
    EG, PG = 4, E // 4
    NBLK = T // BANK
    TB = BANK // P
    SCALE = float(HD) ** -0.5
    NPART = len(Q_PARTS)
    KROWS = NPART * HD
    NGRP = NB * NG
    KT = SEQ // P
    QB = SEQ // BANK
    STEPS = QB * KT
    UNITS = STEPS * REP
    MX_FIRST, MX_PER = 3, 6
    WA = D + 2 * KV + E
    VR = KV + E
    WE = KC * I * 2 + D

    x_t = x.rearrange("b s d -> (b s) d").rearrange("(t p) d -> p t d", p=P)
    out_t = out.rearrange("b s d -> (b s) d").rearrange("(t p) d -> p t d", p=P)
    q_parts = nc.dram_tensor("q_parts", [3, D, T], BF16, kind="Internal").ap()
    k_parts = nc.dram_tensor("k_parts", [3, KV, T], BF16, kind="Internal").ap()
    attn_num = nc.dram_tensor("attn_num", [D, T], F32, kind="Internal").ap()
    attn_sum = nc.dram_tensor("attn_sum", [D, T], F32, kind="Internal").ap()

    with ExitStack() as ctx:
        def sb(name, shape, dt, scope=ctx):
            return scope.enter_context(nc.sbuf_tensor(name, shape, dt))

        def sem(name):
            return ctx.enter_context(nc.semaphore(name))

        banks = [ctx.enter_context(nc.psum_tensor(f"bank{i}", [P, BANK], F32)) for i in range(8)]

        X = sb("X", [P, NT, D], F32)
        xT_hi = sb("xT_hi", [P, KC, T], F32R)
        xT_lo = sb("xT_lo", [P, KC, T], F32R)
        V_all = sb("V_all", [P, NT, NG, 2 * HD], F32)
        logits = sb("logits", [P, NT, E], F32)
        scores = sb("scores", [P, NT, E], F32)
        combine = sb("combine", [P, NT, E], F32)
        ident = sb("ident", [P, P], F32)
        ident_bf = sb("ident_bf", [P, P], BF16)
        bias_sb = sb("bias_sb", [P, E], F32)
        earlier = sb("earlier", [P, EG, EG], F32)
        wo_hi = sb("wo_hi", [P, KC, D], F32R)
        wo_lo = sb("wo_lo", [P, KC, D], F32R)

        sa = ExitStack()
        wa = sb("wa", [P, KC, WA], F32, sa)
        wa_hi = sb("wa_hi", [P, KC, WA], F32R, sa)
        wa_lo = sb("wa_lo", [P, KC, WA], F32R, sa)
        wo_sb = sb("wo_sb", [P, KC, D], F32, sa)
        xn = sb("xn", [P, TB, D], F32, sa)
        stats = sb("stats", [P, NT, 6], F32, sa)
        mv = sb("mv", [P, NT, 2], F32, sa)
        var_eps = sb("var_eps", [P, NT], F32, sa)
        std = sb("std", [P, NT], F32, sa)
        rstd0 = sb("rstd0", [P, NT], F32, sa)
        newton = sb("newton", [P, NT], F32, sa)
        rstd = sb("rstd", [P, NT], F32, sa)
        part = [[sb(f"part{i}_{j}", [P, 2, BANK], BF16, sa) for j in range(3)] for i in range(3)]
        rest = [sb(f"rest_{j}", [P, BANK], F32, sa) for j in range(3)]
        sa.close()
        sc = ExitStack()
        num_sb = sb("num_sb", [P, 2, KC, BANK], F32, sc)
        den_sb = sb("den_sb", [P, 2, KC, BANK], F32, sc)
        attn = sb("attn", [P, KC, BANK], F32, sc)
        attn_hi = sb("attn_hi", [P, KC, BANK], F32R, sc)
        attn_lo = sb("attn_lo", [P, KC, BANK], F32R, sc)
        choice = sb("choice", [P, NT, EG, PG], F32, sc)
        work1 = sb("work1", [P, NT, E], F32, sc)
        work2 = sb("work2", [P, NT, E], F32, sc)
        work3 = sb("work3", [P, NT, E], F32, sc)
        top8 = sb("top8", [P, NT, 8], F32, sc)
        gsc = sb("gsc", [P, NT, EG], F32, sc)
        small = sb("small", [P, 4, NT, EG], F32, sc)
        cnt = sb("cnt", [P, 3, NT], F32, sc)
        sc.close()
        sa2 = ExitStack()
        hold = sb("hold", [P, 10700], F32, sa2)
        bb = ExitStack()
        QS = [sb(f"QS{p}", [P, REP, SEQ], BF16, bb) for p in range(2)]
        KS = [sb(f"KS{p}", [P, SEQ], BF16, bb) for p in range(2)]
        V = [sb(f"V{p}", [P, KT, 2 * HD], F32, bb) for p in range(2)]
        probs = [sb(f"probs{p}", [P, REP, BANK], F32, bb) for p in range(2)]
        O_sb = sb("O_sb", [P, QB, BANK], F32, bb)
        umax = sb("umax", [P, UNITS], F32, bb)
        qmax = sb("qmax", [P, UNITS // 2], F32, bb)
        mrest = sb("mrest", [P, UNITS // 2], F32, bb)
        mparts = sb("mparts", [P, 3, UNITS // 2], BF16, bb)
        mrows = sb("mrows", [3 * UNITS // 2, P], BF16, bb)
        bb.close()
        se = ExitStack()
        w_raw = [sb(f"w_raw{p}", [P, WE], F32, se) for p in range(2)]
        w_hi = [sb(f"w_hi{p}", [P, WE], F32R, se) for p in range(2)]
        w_lo = [sb(f"w_lo{p}", [P, WE], F32R, se) for p in range(2)]
        act_g = [sb(f"act_g{p}", [P, BANK], F32, se) for p in range(2)]
        h = [sb(f"h{p}", [P, BANK], F32, se) for p in range(2)]
        h_hi = [sb(f"h_hi{p}", [P, BANK], F32R, se) for p in range(2)]
        h_lo = [sb(f"h_lo{p}", [P, BANK], F32R, se) for p in range(2)]
        se.close()
        sa2.close()

        x_loaded = [sem(f"x_loaded{c}") for c in range(NBLK)]
        w_loaded = sem("w_loaded")
        consts = sem("consts")
        wa_hi_done, wa_lo_done = sem("wa_hi_done"), sem("wa_lo_done")
        ln_step = sem("ln_step")
        ve_done, std_done, xn_done = sem("ve_done"), sem("std_done"), sem("xn_done")
        tp_done, hi_done, lo_done = sem("tp_done"), sem("hi_done"), sem("lo_done")
        qk_done, vr_done, vr_read = sem("qk_done"), sem("vr_done"), sem("vr_read")
        p1_done, rest_done, p2_done, p3_done = sem("p1_done"), sem("rest_done"), sem("p2_done"), sem("p3_done")
        parts_stored = [sem("parts_stored0"), sem("parts_stored1")]
        stacks_loaded, negmax_loaded = sem("stacks_loaded"), sem("negmax_loaded")
        v_loaded = [sem("v_loaded0"), sem("v_loaded1")]
        mx_done, mx_read = sem("mx_done"), sem("mx_read")
        chain = sem("chain")
        mparts_done, mT_done, mrows_done = sem("mparts_done"), sem("mT_done"), sem("mrows_done")
        st_done, exp_done, pv_done = sem("st_done"), sem("exp_done"), sem("pv_done")
        o_done, o_stored = sem("o_done"), sem("o_stored")
        scores_done, route = sem("scores_done"), sem("route")
        attn_loaded = [sem("attn_loaded0"), sem("attn_loaded1")]
        rden_done, attn_done, ahi_done, alo_done = sem("rden_done"), sem("attn_done"), sem("ahi_done"), sem("alo_done")
        y_done, acc_done = sem("y_done"), sem("acc_done")
        we_loaded = [sem("we_loaded0"), sem("we_loaded1")]
        whi_done, wlo_done = sem("whi_done"), sem("wlo_done")
        g_done, u_done, silu_done = sem("g_done"), sem("u_done"), sem("silu_done")
        h_done, hhi_done, hlo_done = sem("h_done"), sem("hhi_done"), sem("hlo_done")
        stored = sem("stored")

        EXP0 = UNITS
        PV0 = 2
        O0 = 2

        def ring_before(u):
            if u >= 3:
                return u - 2
            return max(v for v in range(UNITS) if v % 3 == u) + 1 - UNITS

        def mx_units(step):
            lo = (step - MX_FIRST) * MX_PER
            return range(max(lo, 0), min(max(lo + MX_PER, 0), UNITS)) if step >= MX_FIRST else range(0)

        def three(pe, psum, lhs, rhs):
            terms = [(l, r) for (lh, ll), (rh, rl) in zip(lhs, rhs) for l, r in ((lh, rh), (lh, rl), (ll, rh))]
            for i, (l, r) in enumerate(terms):
                last = pe.matmul(psum, l, r, start=(i == 0), stop=(i == len(terms) - 1))
            return last

        block = ctx.enter_context(nc.Block())

        @block.sync
        def _(sp):
            for c in range(NBLK):
                sp.dma_start(X[:, TB * c:TB * (c + 1), :], x_t[:, TB * c:TB * (c + 1), :]).then_inc(x_loaded[c], 16)
            for n in range(NBLK):
                for j in range(3):
                    M = P if j < 2 else KV
                    dst = q_parts[:, P * j:P * (j + 1), :] if j < 2 else k_parts
                    for i in range(3):
                        sp.wait_ge((p1_done, p2_done, p3_done)[i], 3 * n + j + 1)
                        sp.dma_start(dst[i, :, BANK * n:BANK * (n + 1)],
                                     part[i][j][0:M, n % 2, :]).then_inc(parts_stored[n % 2], 16)

            def load_stacks(b, g, p):
                q0, t0 = g * (REP * HD), b * SEQ
                for s, (i, j) in enumerate(zip(Q_PARTS, K_PARTS)):
                    sp.dma_start(QS[p][HD * s:HD * (s + 1), :, :],
                                 q_parts[i, bass.ds(q0, REP * HD), bass.ds(t0, SEQ)].rearrange("(h d) t -> d h t", d=HD)
                                 ).then_inc(stacks_loaded, 16)
                    sp.dma_start(KS[p][HD * s:HD * (s + 1), :],
                                 k_parts[j, bass.ds(g * HD, HD), bass.ds(t0, SEQ)]).then_inc(stacks_loaded, 16)

            def load_v(b, g, p):
                sp.dma_start(V[p][:, :, :], V_all[:, bass.ds(b * KT, KT), bass.ds(g, 1), :].rearrange("p t g d -> p t (g d)")
                             ).then_inc(v_loaded[p], 16)

            def negmax(n, p):
                sp.wait_ge(mrows_done, n + 1)
                sp.dma_start(QS[p][KROWS:KROWS + 3, :, :].rearrange("a h (t q) -> a (h t) q", q=P),
                             mrows[:, :]).then_inc(negmax_loaded, 16)

            for p in range(2):
                sp.wait_ge(parts_stored[p], 16 * 9 * NBLK // 2)
            sp.wait_ge(vr_read, 2 * NBLK)
            sp.wait_ge(consts, 4)
            load_stacks(0, 0, 0)
            load_v(0, 0, 0)
            sp.wait_ge(stacks_loaded, 16 * 2 * NPART)
            load_stacks(0, 1, 1)
            load_v(0, 1, 1)
            negmax(0, 0)

            def group_io(b, half, p, nb=None, nhalf=None, more_max=True):
                n = b * NG + half * 2 + p
                if more_max:
                    negmax(n + 1, 1 - p)
                if nb is not None:
                    sp.wait_ge(st_done, UNITS * n + UNITS)
                    for par in range(2):
                        sp.wait_ge(parts_stored[par], 16 * 9 * NBLK // 2)
                    load_stacks(nb, nhalf * 2 + p, p)
                    sp.wait_ge(pv_done, STEPS * n + STEPS + PV0)
                    sp.wait_ge(vr_read, 2 * NBLK)
                    load_v(nb, nhalf * 2 + p, p)

            with sp.Fori(0, NB - 1) as b:
                for half in range(2):
                    for p in range(2):
                        group_io(b, half, p, b + half, 1 - half)
            b = NB - 1
            for p in range(2):
                group_io(b, 0, p, b, 1)
            group_io(b, 1, 0)
            group_io(b, 1, 1, more_max=False)

            sp.wait_ge(o_stored, 16 * 2 * REP * NGRP)
            num_v = attn_num.rearrange("(k p) t -> p k t", p=P)
            den_v = attn_sum.rearrange("(k p) t -> p k t", p=P)

            def load_attn(n):
                sp.dma_start(num_sb[:, n % 2, :, :], num_v[:, :, BANK * n:BANK * (n + 1)]).then_inc(attn_loaded[n % 2], 16)
                sp.dma_start(den_sb[:, n % 2, :, :], den_v[:, :, BANK * n:BANK * (n + 1)]).then_inc(attn_loaded[n % 2], 16)

            def load_expert(e, p):
                w = w_raw[p]
                sp.dma_start(w[:, 0:KC * I].rearrange("p (k i) -> p k i", k=KC),
                             wg[bass.ds(e, 1), :, :].rearrange("e (k p) i -> p (e k) i", p=P)).then_inc(we_loaded[p], 16)
                sp.dma_start(w[:, KC * I:2 * KC * I].rearrange("p (k i) -> p k i", k=KC),
                             wu[bass.ds(e, 1), :, :].rearrange("e (k p) i -> p (e k) i", p=P)).then_inc(we_loaded[p], 16)
                sp.dma_start(w[:, 2 * KC * I:WE],
                             wd[bass.ds(e, 1), :, :].rearrange("e i d -> i (e d)")).then_inc(we_loaded[p], 16)

            load_attn(0)
            load_attn(1)
            load_expert(0, 0)
            load_expert(1, 1)
            for n in range(2, NBLK):
                sp.wait_ge(attn_done, n - 1)
                load_attn(n)
            with sp.Fori(0, E // 2 - 1) as i:
                for p in range(2):
                    sp.wait_ge(whi_done, 2 * i + p + 1)
                    sp.wait_ge(wlo_done, 2 * i + p + 1)
                    load_expert(2 * i + 2 + p, p)
            for n in range(NBLK):
                sp.wait_ge(acc_done, NT + TB * ((E - 1) * NBLK + n + 1))
                sp.dma_start(out_t[:, TB * n:TB * (n + 1), :], X[:, TB * n:TB * (n + 1), :]).then_inc(stored, 16)
            sp.wait_ge(stored, 16 * NBLK)

        @block.gpsimd
        def _(pool):
            pool.memset(ident[:, :], 0.0).then_inc(consts, 1)
            pool.memset(earlier[:, :, :], 1.0).then_inc(consts, 1)
            pool.memset(V_all[:, :, :, HD:2 * HD], 1.0).then_inc(consts, 1)
            pool.wait_ge(consts, 3)
            pool.affine_select(out=ident[:, :], in_=ident[:, :], compare_op=ALU.not_equal, fill=1.0, base=0,
                               pattern=[[-1, P]], channel_multiplier=1).then_inc(consts, 1)
            pool.affine_select(out=earlier[:, :, :], in_=earlier[:, :, :], compare_op=ALU.is_gt, fill=0.0, base=0,
                               pattern=[[1, EG], [-1, EG]], channel_multiplier=0).then_inc(consts, 1)
            for n in range(NBLK):
                for j in range(3):
                    M = P if j < 2 else KV
                    u = 3 * n + j
                    if n >= 2:
                        pool.wait_ge(parts_stored[n % 2], 16 * 9 * (n // 2))
                    pool.wait_ge(p2_done, u + 1)
                    pool.wait_ge(rest_done, u + 1)
                    pool.tensor_tensor(part[2][j][0:M, n % 2, :], rest[j][0:M, :], part[1][j][0:M, n % 2, :],
                                       ALU.subtract).then_inc(p3_done, 1)
            def store(n, b, g):
                pool.wait_ge(o_done, 2 * n + 2 + O0)
                for r in range(REP):
                    rows = bass.ds(g * (REP * HD) + r * HD, HD)
                    for dst, at in ((attn_num, 2 * HD * r), (attn_sum, 2 * HD * r + HD)):
                        pool.dma_start(dst[rows, bass.ds(b * SEQ, SEQ)],
                                     O_sb[at:at + HD, :, :]).then_inc(o_stored, 16)

            with pool.Fori(0, NB) as b:
                for g in range(NG):
                    store(b * NG + g, b, g)

            for n in range(NBLK):
                pool.wait_ge(attn_loaded[n % 2], 32 * (n // 2 + 1))
                pool.wait_ge(rden_done, n + 1)
                if n >= 1:
                    pool.wait_ge(ahi_done, n)
                    pool.wait_ge(alo_done, n)
                pool.tensor_tensor(attn[:, :, :], num_sb[:, n % 2, :, :], den_sb[:, n % 2, :, :], ALU.mult).then_inc(attn_done, 1)

        @block.scalar
        def _(act):
            act.dma_start(wa[:, :, 0:D], wq.rearrange("(k p) n -> p k n", p=P)).then_inc(w_loaded, 16)
            act.dma_start(wa[:, :, D:D + KV], wk.rearrange("(k p) n -> p k n", p=P)).then_inc(w_loaded, 16)
            act.dma_start(wa[:, :, D + KV:D + 2 * KV], wv.rearrange("(k p) n -> p k n", p=P)).then_inc(w_loaded, 16)
            act.dma_start(wa[:, :, D + 2 * KV:WA], wr.rearrange("(k p) n -> p k n", p=P)).then_inc(w_loaded, 16)
            act.dma_start(wo_sb[:, :, :], wo.rearrange("(k p) n -> p k n", p=P)).then_inc(w_loaded, 16)
            act.dma_start(bias_sb[:, :], bias.rearrange("(a n) -> a n", a=1).broadcast_to([P, E])).then_inc(w_loaded, 16)

            def root(c):
                act.wait_ge(ve_done, c + 1)
                act.activation(std[:, TB * c:TB * (c + 1)], var_eps[:, TB * c:TB * (c + 1)], ACT.Sqrt).then_inc(std_done, 1)

            root(0)
            act.wait_ge(w_loaded, 96)
            act.activation(wa_hi[:, :, :], wa[:, :, :], ACT.Copy).then_inc(wa_hi_done, 1)
            act.activation(wo_hi[:, :, :], wo_sb[:, :, :], ACT.Copy).then_inc(wa_hi_done, 1)
            for c in range(NBLK):
                if c + 1 < NBLK:
                    root(c + 1)
                for q in range(2 * c, 2 * c + 2):
                    act.wait_ge(tp_done, q + 1)
                    act.activation(xT_hi[:, :, 2 * P * q:2 * P * (q + 1)],
                                   banks[q % 2][:, :].rearrange("p (k t) -> p k t", k=KC), ACT.Copy).then_inc(hi_done, 1)
                for j in range(3):
                    M = P if j < 2 else KV
                    u = 3 * c + j
                    if c >= 2:
                        act.wait_ge(parts_stored[c % 2], 16 * 9 * (c // 2))
                    act.wait_ge(qk_done, u + 1)
                    act.activation(part[0][j][0:M, c % 2, :], banks[2 + j][0:M, :], ACT.Copy).then_inc(p1_done, 1)
                    act.wait_ge(rest_done, u + 1)
                    act.activation(part[1][j][0:M, c % 2, :], rest[j][0:M, :], ACT.Copy).then_inc(p2_done, 1)
                act.wait_ge(vr_done, c + 1)
                vr = banks[5 + c % 2][:, 0:TB * VR].rearrange("p (t n) -> p t n", t=TB)
                act.activation(V_all[:, TB * c:TB * (c + 1), :, 0:HD],
                               vr[:, :, 0:KV].rearrange("p t (g d) -> p t g d", d=HD), ACT.Copy).then_inc(vr_read, 1)
                act.activation(logits[:, TB * c:TB * (c + 1), :], vr[:, :, KV:VR], ACT.Copy).then_inc(vr_read, 1)
            act.wait_ge(vr_read, 2 * NBLK)
            act.activation(scores[:, :, :], logits[:, :, :], ACT.Sigmoid).then_inc(scores_done, 1)

            def exps(n):
                for s in range(STEPS):
                    for r in range(REP):
                        u = REP * s + r
                        if r == 0:
                            act.wait_ge(pv_done, STEPS * n + s - 1 + PV0)
                        act.wait_ge(st_done, UNITS * n + u + 1)
                        act.activation(probs[s % 2][:, r, :], banks[u % 3][:, :], ACT.Exp, scale=SCALE).then_inc(exp_done, 1)

            with act.Fori(0, NGRP) as n:
                exps(n)

            for n in range(NBLK):
                act.wait_ge(attn_done, n + 1)
                if n >= 1:
                    act.wait_ge(y_done, 2 * n)
                act.activation(attn_hi[:, :, :], attn[:, :, :], ACT.Copy).then_inc(ahi_done, 1)

            def w_split(p, loads):
                act.wait_ge(we_loaded[p], loads)
                act.activation(w_hi[p][:, :], w_raw[p][:, :], ACT.Copy).then_inc(whi_done, 1)

            def silu(k, par, first=False):
                act.wait_ge(g_done, k + 1)
                if not first:
                    act.wait_ge(h_done, k - 1)
                act.activation(act_g[par][:, :], banks[par][:, :], ACT.Silu).then_inc(silu_done, 1)

            def hi_of_h(k, par, first=False):
                act.wait_ge(h_done, k + 1)
                if not first:
                    act.wait_ge(y_done, 2 * (k - 1) + 2 * NBLK)
                act.activation(h_hi[par][:, :], h[par][:, :], ACT.Copy).then_inc(hhi_done, 1)

            w_split(0, 48)
            silu(0, 0, True)
            hi_of_h(0, 0, True)

            def expert_pair(i, last):
                for p in range(2):
                    for j in range(NBLK):
                        k = 2 * NBLK * i + NBLK * p + j
                        final = last and p == 1
                        if j == 1 and not final:
                            act.wait_ge(y_done, 2 * (2 * NBLK * i + NBLK * p) + 2 * NBLK)
                            w_split(1 - p, 48 * i + 48 * p + 48)
                        if not (final and j == NBLK - 1):
                            silu(k + 1, (j + 1) % 2)
                            hi_of_h(k + 1, (j + 1) % 2)

            with act.Fori(0, E // 2 - 1) as i:
                expert_pair(i, False)
            expert_pair(E // 2 - 1, True)

        @block.vector
        def _(dve):
            dve.memset(KS[0][KROWS:P, :], 1.0).then_inc(exp_done, EXP0)
            dve.memset(KS[1][KROWS:P, :], 1.0).then_inc(pv_done, PV0)
            dve.memset(cnt[:, 0, :], 0.0).then_inc(o_done, O0)
            step = [0]

            def link(ins, s=ln_step):
                ins.then_inc(s, 1)
                step[0] += 1
                dve.wait_ge(s, step[0])

            def ln_stats(c):
                tiles = range(TB * c, TB * (c + 1))
                sl = slice(TB * c, TB * (c + 1))
                dve.wait_ge(x_loaded[c], 16)
                for t in tiles:
                    last = dve.bn_stats(stats[:, t, :], X[:, t, :])
                link(last)
                for t in tiles:
                    last = dve.bn_aggr(mv[:, t, :], stats[:, t, :])
                link(last)
                dve.tensor_scalar(var_eps[:, sl], mv[:, sl, 1], LN_EPS, None, ALU.add).then_inc(ve_done, 1)

            def ln_apply(c):
                sl = slice(TB * c, TB * (c + 1))
                dve.wait_ge(std_done, c + 1)
                dve.wait_ge(ve_done, c + 1)
                link(dve.reciprocal(rstd0[:, sl], std[:, sl]))
                link(dve.tensor_tensor(newton[:, sl], rstd0[:, sl], rstd0[:, sl], ALU.mult))
                link(dve.tensor_tensor(newton[:, sl], newton[:, sl], var_eps[:, sl], ALU.mult))
                link(dve.tensor_scalar(newton[:, sl], newton[:, sl], -0.5, 1.5, ALU.mult, ALU.add))
                link(dve.tensor_tensor(rstd[:, sl], rstd0[:, sl], newton[:, sl], ALU.mult))
                for i in range(TB):
                    t = TB * c + i
                    if c >= 1:
                        dve.wait_ge(tp_done, 2 * (c - 1) + i // 2 + 1)
                    dve.tensor_scalar(xn[:, i, :], X[:, t, :], mv[:, t, 0:1], rstd[:, t:t + 1],
                                      ALU.subtract, ALU.mult).then_inc(xn_done, 1)

            ln_stats(0)
            dve.wait_ge(consts, 5)
            dve.tensor_copy(ident_bf[:, :], ident[:, :]).then_inc(consts, 1)
            ln_stats(1)
            ln_apply(0)
            dve.wait_ge(wa_hi_done, 2)
            dve.tensor_tensor(wa_lo[:, :, :], wa[:, :, :], wa_hi[:, :, :].bitcast(F32), ALU.subtract).then_inc(wa_lo_done, 1)
            dve.tensor_tensor(wo_lo[:, :, :], wo_sb[:, :, :], wo_hi[:, :, :].bitcast(F32), ALU.subtract).then_inc(wa_lo_done, 1)
            for c in range(NBLK):
                if c + 2 < NBLK:
                    ln_stats(c + 2)
                if c + 1 < NBLK:
                    ln_apply(c + 1)
                for q in range(2 * c, 2 * c + 2):
                    dve.wait_ge(hi_done, q + 1)
                    cols = slice(2 * P * q, 2 * P * (q + 1))
                    dve.tensor_tensor(xT_lo[:, :, cols], banks[q % 2][:, :].rearrange("p (k t) -> p k t", k=KC),
                                      xT_hi[:, :, cols].bitcast(F32), ALU.subtract).then_inc(lo_done, 1)
                for j in range(3):
                    M = P if j < 2 else KV
                    u = 3 * c + j
                    dve.wait_ge(p1_done, u + 1)
                    if c >= 1:
                        dve.wait_ge(p3_done, u - 2)
                    dve.tensor_tensor(rest[j][0:M, :], banks[2 + j][0:M, :], part[0][j][0:M, c % 2, :],
                                      ALU.subtract).then_inc(rest_done, 1)

            def maxima(n):
                for u in range(UNITS):
                    dve.wait_ge(mx_done, UNITS * n + u + 1)
                    dve.tensor_reduce(umax[:, u:u + 1], banks[3 + u % 3][:, :], AX_X, ALU.max).then_inc(mx_read, 1)
                dve.wait_ge(mx_read, UNITS * n + UNITS)
                dve.tensor_reduce(qmax[:, :], umax[:, :].rearrange("p (q h) -> p q h", h=2), AX_X, ALU.max).then_inc(chain, 1)
                dve.wait_ge(chain, 4 * n + 1)
                dve.tensor_scalar(mparts[:, 0, :], qmax[:, :], -1.0, None, ALU.mult).then_inc(chain, 1)
                dve.wait_ge(chain, 4 * n + 2)
                dve.scalar_tensor_tensor(out=mrest[:, :], in0=qmax[:, :], scalar=-1.0, in1=mparts[:, 0, :],
                                         op0=ALU.mult, op1=ALU.subtract).then_inc(chain, 1)
                dve.wait_ge(chain, 4 * n + 3)
                dve.tensor_copy(mparts[:, 1, :], mrest[:, :]).then_inc(chain, 1)
                dve.wait_ge(chain, 4 * n + 4)
                dve.tensor_tensor(mparts[:, 2, :], mrest[:, :], mparts[:, 1, :], ALU.subtract).then_inc(mparts_done, 1)
                dve.wait_ge(mT_done, n + 1)
                dve.wait_ge(negmax_loaded, 16 * n)
                dve.tensor_copy(mrows[:, :], banks[5][0:3 * UNITS // 2, 0:P // 2].bitcast(BF16)).then_inc(mrows_done, 1)

            def outputs(n):
                for qb in range(QB):
                    dve.wait_ge(pv_done, STEPS * n + KT * (qb + 1) + PV0)
                    dve.wait_ge(o_stored, 16 * 2 * REP * n)
                    dve.tensor_copy(O_sb[:, qb, :], banks[6 + qb][:, :]).then_inc(o_done, 1)

            maxima(0)
            with dve.Fori(0, NGRP - 1) as n:
                maxima(n + 1)
                outputs(n)

            step[0] = 0
            r_ = lambda ins: link(ins, route)
            dve.wait_ge(scores_done, 1)
            sc4 = scores[:, :, :].rearrange("p t (g e) -> p t g e", g=EG)
            b4 = bias_sb[:, :].rearrange("p (a g e) -> p a g e", a=1, g=EG).broadcast_to([P, NT, EG, PG])
            r_(dve.tensor_tensor(choice[:, :, :, :], sc4, b4, ALU.add))
            c_lo, c_hi = choice[:, :, :, 0:PG:2], choice[:, :, :, 1:PG:2]
            pair_max = work1[:, :, 0:2 * EG].rearrange("p t (g e) -> p t g e", g=EG)
            pair_min = work2[:, :, 0:2 * EG].rearrange("p t (g e) -> p t g e", g=EG)
            r_(dve.tensor_tensor(pair_max, c_lo, c_hi, ALU.max))
            r_(dve.tensor_tensor(pair_min, c_lo, c_hi, ALU.min))
            first, second, third = small[:, 0, :, :], small[:, 1, :, :], small[:, 2, :, :]
            r_(dve.tensor_tensor(first, pair_max[:, :, :, 0], pair_max[:, :, :, 1], ALU.max))
            r_(dve.tensor_tensor(second, pair_max[:, :, :, 0], pair_max[:, :, :, 1], ALU.min))
            r_(dve.tensor_tensor(third, pair_min[:, :, :, 0], pair_min[:, :, :, 1], ALU.max))
            r_(dve.tensor_tensor(second, second, third, ALU.max))
            r_(dve.tensor_tensor(gsc[:, :, :], first, second, ALU.add))
            other = gsc[:, :, :].unsqueeze(2).broadcast_to([P, NT, EG, EG])
            own = gsc[:, :, :].unsqueeze(3).broadcast_to([P, NT, EG, EG])
            more = work1[:, :, :].rearrange("p t (g e) -> p t g e", g=EG)
            same = work2[:, :, :].rearrange("p t (g e) -> p t g e", g=EG)
            lower = earlier[:, :, :].unsqueeze(1).broadcast_to([P, NT, EG, EG])
            r_(dve.tensor_tensor(more, other, own, ALU.is_gt))
            r_(dve.tensor_tensor(same, other, own, ALU.is_equal))
            r_(dve.tensor_tensor(same, same, lower, ALU.mult))
            r_(dve.tensor_tensor(more, more, same, ALU.add))
            rank, keep, drop = small[:, 0, :, :], small[:, 1, :, :], small[:, 2, :, :]
            r_(dve.tensor_reduce(rank, more, AX_X, ALU.add))
            r_(dve.tensor_scalar(keep, rank, 2.0, None, ALU.is_lt))
            r_(dve.tensor_scalar(drop, keep, -NEG_INF, NEG_INF, ALU.mult, ALU.add))
            wide = lambda a: a.unsqueeze(3).broadcast_to([P, NT, EG, PG])
            r_(dve.tensor_tensor(choice[:, :, :, :], choice[:, :, :, :], wide(keep), ALU.mult))
            r_(dve.tensor_tensor(choice[:, :, :, :], choice[:, :, :, :], wide(drop), ALU.add))
            masked = choice[:, :, :, :].rearrange("p t g e -> p t (g e)")
            for t in range(NT):
                last = dve.max(top8[:, t, :], masked[:, t, :])
            r_(last)
            fourth = top8[:, :, 3:4].broadcast_to([P, NT, E])
            above, equal, run = work1[:, :, :], work2[:, :, :], work3[:, :, :]
            r_(dve.tensor_tensor(above, masked, fourth, ALU.is_gt))
            r_(dve.tensor_tensor(equal, masked, fourth, ALU.is_equal))
            r_(dve.tensor_reduce(cnt[:, 0, :], above, AX_X, ALU.add))
            r_(dve.tensor_scalar(cnt[:, 1, :], cnt[:, 0, :], -1.0, 4.0, ALU.mult, ALU.add))
            src, dst = equal, run
            for d in (1, 2, 4, 8):
                r_(dve.tensor_copy(dst[:, :, 0:d], src[:, :, 0:d]))
                r_(dve.tensor_tensor(dst[:, :, d:E], src[:, :, d:E], src[:, :, 0:E - d], ALU.add))
                if d == 1:
                    src, dst = run, combine[:, :, :]
                else:
                    src, dst = dst, src
            counted, free = src, dst
            r_(dve.tensor_tensor(free, counted, cnt[:, 1, :].unsqueeze(2).broadcast_to([P, NT, E]), ALU.is_le))
            r_(dve.tensor_tensor(free, free, equal, ALU.mult))
            r_(dve.tensor_tensor(above, above, free, ALU.add))
            r_(dve.tensor_tensor(above, above, scores[:, :, :], ALU.mult))
            r_(dve.tensor_reduce(cnt[:, 0, :], above, AX_X, ALU.add))
            r_(dve.tensor_scalar(cnt[:, 0, :], cnt[:, 0, :], 1e-20, None, ALU.add))
            r_(dve.reciprocal(cnt[:, 2, :], cnt[:, 0, :]))
            r_(dve.tensor_scalar(cnt[:, 2, :], cnt[:, 2, :], ROUTED_SCALE, None, ALU.mult))
            r_(dve.tensor_tensor(combine[:, :, :], above, cnt[:, 2, :].unsqueeze(2).broadcast_to([P, NT, E]), ALU.mult))
            outputs(NGRP - 1)

            def inverse(n):
                dve.wait_ge(attn_loaded[n % 2], 32 * (n // 2 + 1))
                dve.reciprocal(den_sb[:, n % 2, :, :], den_sb[:, n % 2, :, :]).then_inc(rden_done, 1)

            inverse(0)
            for n in range(NBLK):
                dve.wait_ge(ahi_done, n + 1)
                if n >= 1:
                    dve.wait_ge(y_done, 2 * n)
                dve.tensor_tensor(attn_lo[:, :, :], attn[:, :, :], attn_hi[:, :, :].bitcast(F32), ALU.subtract).then_inc(alo_done, 1)
                if n + 1 < NBLK:
                    inverse(n + 1)
                for t in range(TB):
                    dve.wait_ge(y_done, 2 * n + t // 2 + 1)
                    xt = X[:, TB * n + t, :]
                    dve.tensor_tensor(xt, banks[4 + 2 * (n % 2) + t // 2][:, D * (t % 2):D * (t % 2 + 1)], xt,
                                      ALU.add).then_inc(acc_done, 1)

            def w_split(p, count):
                dve.wait_ge(whi_done, count)
                dve.tensor_tensor(w_lo[p][:, :], w_raw[p][:, :], w_hi[p][:, :].bitcast(F32), ALU.subtract).then_inc(wlo_done, 1)

            def gated(k, par, first=False):
                dve.wait_ge(u_done, k + 1)
                dve.wait_ge(silu_done, k + 1)
                if not first:
                    dve.wait_ge(hhi_done, k - 1)
                    dve.wait_ge(hlo_done, k - 1)
                dve.tensor_tensor(h[par][:, :], banks[2 + par][:, :], act_g[par][:, :], ALU.mult).then_inc(h_done, 1)
                dve.wait_ge(hhi_done, k + 1)
                dve.tensor_tensor(h_lo[par][:, :], h[par][:, :], h_hi[par][:, :].bitcast(F32), ALU.subtract).then_inc(hlo_done, 1)

            def add_expert(k, j, e):
                for t in range(TB):
                    dve.wait_ge(y_done, 2 * NBLK + 2 * k + t // 2 + 1)
                    dve.wait_ge(acc_done, TB * k + t + 1)
                    tile = TB * j + t
                    dve.scalar_tensor_tensor(out=X[:, tile, :], in0=banks[4 + 2 * (j % 2) + t // 2][:, D * (t % 2):D * (t % 2 + 1)],
                                             scalar=combine[:, tile, bass.ds(e, 1)], in1=X[:, tile, :],
                                             op0=ALU.mult, op1=ALU.add).then_inc(acc_done, 1)

            w_split(0, 1)
            gated(0, 0, True)

            def expert_pair(i, last):
                for p in range(2):
                    for j in range(NBLK):
                        k = 2 * NBLK * i + NBLK * p + j
                        final = last and p == 1
                        if j == 1 and not final:
                            w_split(1 - p, 2 * i + p + 2)
                        if not (final and j == NBLK - 1):
                            gated(k + 1, (j + 1) % 2)
                        add_expert(k, j, 2 * i + p)

            with dve.Fori(0, E // 2 - 1) as i:
                expert_pair(i, False)
            expert_pair(E // 2 - 1, True)

        @block.tensor
        def _(pe):
            def transposes(c):
                for q in range(2 * c, 2 * c + 2):
                    if q >= 2:
                        pe.wait_ge(lo_done, q - 1)
                    for t in range(2):
                        pe.wait_ge(xn_done, 2 * q + t + 1)
                        for k in range(KC):
                            at = 2 * P * k + P * t
                            last = pe.transpose(banks[q % 2][:, at:at + P], xn[:, (2 * q + t) % TB, P * k:P * (k + 1)], ident[:, :])
                    last.then_inc(tp_done, 1)

            def xT(k, sl):
                return xT_hi[:, k, sl], xT_lo[:, k, sl]

            def project(c):
                sl = slice(BANK * c, BANK * (c + 1))
                pe.wait_ge(lo_done, 2 * c + 2)
                if c == 0:
                    pe.wait_ge(wa_lo_done, 2)
                for j in range(3):
                    if c >= 1:
                        pe.wait_ge(rest_done, 3 * (c - 1) + j + 1)
                    M = P if j < 2 else KV
                    lhs = [(wa_hi[:, k, P * j:P * j + M], wa_lo[:, k, P * j:P * j + M]) for k in range(KC)]
                    three(pe, banks[2 + j][0:M, :], lhs, [xT(k, sl) for k in range(KC)]).then_inc(qk_done, 1)
                if c >= 2:
                    pe.wait_ge(vr_read, 2 * (c - 1))
                for t in range(TB):
                    at = BANK * c + P * t
                    rhs = [(wa_hi[:, k, D + KV:WA], wa_lo[:, k, D + KV:WA]) for k in range(KC)]
                    last = three(pe, banks[5 + c % 2][:, VR * t:VR * (t + 1)], [xT(k, slice(at, at + P)) for k in range(KC)], rhs)
                last.then_inc(vr_done, 1)

            pe.wait_ge(consts, 6)
            transposes(0)
            for c in range(NBLK):
                if c + 1 < NBLK:
                    transposes(c + 1)
                project(c)

            def max_unit(n, p, u):
                hq, half = u // 2, u % 2
                head, qt = hq // KT, hq % KT
                if isinstance(n, int) and n == 0:
                    if u >= 3:
                        pe.wait_ge(mx_read, ring_before(u))
                else:
                    pe.wait_ge(mx_read, UNITS * n + ring_before(u))
                pe.matmul(banks[3 + u % 3][:, :], QS[p][0:KROWS, head, P * qt:P * (qt + 1)],
                          KS[p][0:KROWS, BANK * half:BANK * (half + 1)], start=True, stop=True).then_inc(mx_done, 1)

            def turn_maxima(n):
                pe.wait_ge(mparts_done, n + 1)
                pe.transpose(banks[5][0:3 * UNITS // 2, 0:P // 2].bitcast(BF16),
                             mparts[:, :, :].rearrange("p a q -> p (a q)"), ident_bf[:, :]).then_inc(mT_done, 1)

            def values(n, p, s):
                qb, kt = s // KT, s % KT
                pe.wait_ge(exp_done, UNITS * n + REP * (s + 1) + EXP0)
                if kt == 0:
                    pe.wait_ge(o_done, 2 * n + qb - 1 + O0)
                if s == 0:
                    pe.wait_ge(v_loaded[p], 8 * n - 8 * p + 16)
                for r in range(REP):
                    last = pe.matmul(banks[6 + qb][2 * HD * r:2 * HD * (r + 1), :], V[p][:, kt, :], probs[s % 2][:, r, :],
                                     start=(kt == 0), stop=(kt == KT - 1))
                last.then_inc(pv_done, 1)

            def attend(n, p, more):
                for s in range(STEPS):
                    qb, kt = s // KT, s % KT
                    mx = list(mx_units(s)) if more else []
                    if mx and mx[0] == 0:
                        pe.wait_ge(stacks_loaded, 16 * 2 * NPART * n + 16 * 2 * NPART * 2)
                    for r in range(REP):
                        u = REP * s + r
                        if u == 0:
                            pe.wait_ge(negmax_loaded, 16 * n + 16)
                        pe.wait_ge(exp_done, UNITS * n + ring_before(u) + EXP0)
                        pe.matmul(banks[u % 3][:, :], KS[p][0:KROWS + 3, P * kt:P * (kt + 1)],
                                  QS[p][0:KROWS + 3, r, BANK * qb:BANK * (qb + 1)], start=True, stop=True).then_inc(st_done, 1)
                        if mx and r < 3:
                            max_unit(n + 1, 1 - p, mx.pop(0))
                        if r == 2 and s > 0:
                            values(n, p, s - 1)
                    for u in mx:
                        max_unit(n + 1, 1 - p, u)
                    if more and s == STEPS - 2:
                        turn_maxima(n + 1)
                values(n, p, STEPS - 1)

            pe.wait_ge(stacks_loaded, 16 * 2 * NPART)
            for u in range(UNITS):
                max_unit(0, 0, u)
            turn_maxima(0)
            with pe.Fori(0, NGRP // 2 - 1) as i:
                for p in range(2):
                    attend(2 * i + p, p, True)
            attend(NGRP - 2, 0, True)
            attend(NGRP - 1, 1, False)

            pe.wait_ge(o_done, 2 * NGRP + O0)
            for n in range(NBLK):
                pe.wait_ge(alo_done, n + 1)
                for t in range(TB):
                    if n >= 2 and t % 2 == 0:
                        pe.wait_ge(acc_done, TB * (n - 2) + t + 2)
                    lhs = [(attn_hi[:, k, P * t:P * (t + 1)], attn_lo[:, k, P * t:P * (t + 1)]) for k in range(KC)]
                    rhs = [(wo_hi[:, k, :], wo_lo[:, k, :]) for k in range(KC)]
                    last = three(pe, banks[4 + 2 * (n % 2) + t // 2][:, D * (t % 2):D * (t % 2 + 1)], lhs, rhs)
                    if t % 2:
                        last.then_inc(y_done, 1)

            def gate_up(k, blk, p, par, first=False):
                sl = slice(BANK * blk, BANK * (blk + 1))
                rhs = [xT(c, sl) for c in range(KC)]
                for m, (read, done) in enumerate(((silu_done, g_done), (h_done, u_done))):
                    if not first:
                        pe.wait_ge(read, k - 1)
                    at = KC * I * m
                    lhs = [(w_hi[p][:, at + I * c:at + I * (c + 1)], w_lo[p][:, at + I * c:at + I * (c + 1)]) for c in range(KC)]
                    three(pe, banks[2 * m + par][:, :], lhs, rhs).then_inc(done, 1)

            def down(k, j, p):
                pe.wait_ge(hlo_done, k + 1)
                for t in range(TB):
                    if t % 2 == 0:
                        pe.wait_ge(acc_done, TB * k + NT - 2 * TB + t + 2)
                    sl = slice(P * t, P * (t + 1))
                    at = 2 * KC * I
                    last = three(pe, banks[4 + 2 * (j % 2) + t // 2][:, D * (t % 2):D * (t % 2 + 1)],
                                 [(h_hi[j % 2][:, sl], h_lo[j % 2][:, sl])], [(w_hi[p][:, at:WE], w_lo[p][:, at:WE])])
                    if t % 2:
                        last.then_inc(y_done, 1)

            pe.wait_ge(wlo_done, 1)
            gate_up(0, 0, 0, 0, True)

            def expert_pair(i, last):
                for p in range(2):
                    for j in range(NBLK):
                        k = 2 * NBLK * i + NBLK * p + j
                        final = last and p == 1
                        if not (final and j == NBLK - 1):
                            if j == NBLK - 1:
                                pe.wait_ge(wlo_done, 2 * i + p + 2)
                                gate_up(k + 1, 0, 1 - p, 0)
                            else:
                                gate_up(k + 1, j + 1, p, (j + 1) % 2)
                        down(k, j, p)

            with pe.Fori(0, E // 2 - 1) as i:
                expert_pair(i, False)
            expert_pair(E // 2 - 1, True)


def kernel(L0_attn_x, L0_attn_Wq, L0_attn_Wk, L0_attn_Wv, L0_attn_Wo, L0_ffn_router_weight, L0_ffn_router_bias,
           L0_ffn_w_gate, L0_ffn_w_up, L0_ffn_w_down):
    import numpy as np
    import concourse.bacc as bacc
    from concourse.bass_utils import run_bass_kernel_spmd

    arrays = {
        "x_in": L0_attn_x, "wq_in": L0_attn_Wq, "wk_in": L0_attn_Wk, "wv_in": L0_attn_Wv, "wo_in": L0_attn_Wo,
        "wr_in": np.transpose(L0_ffn_router_weight), "bias_in": L0_ffn_router_bias,
        "wg_in": np.transpose(L0_ffn_w_gate, (0, 2, 1)), "wu_in": np.transpose(L0_ffn_w_up, (0, 2, 1)),
        "wd_in": np.transpose(L0_ffn_w_down, (0, 2, 1)),
    }
    arrays = {name: np.ascontiguousarray(a) for name, a in arrays.items()}
    nc = bacc.Bacc("TRN2", target_bir_lowering=False, num_devices=1)
    ins = [nc.dram_tensor(name, a.shape, mybir.dt.from_np(a.dtype), kind="ExternalInput").ap() for name, a in arrays.items()]
    out = nc.dram_tensor("out", arrays["x_in"].shape, F32, kind="ExternalOutput").ap()
    build_layer(nc, *ins, out)
    result = run_bass_kernel_spmd(nc, [arrays], core_ids=[0])
    return result.results[0]["out"]
```

```python
from contextlib import ExitStack

import concourse.bass as bass
from concourse import mybir

F32 = mybir.dt.float32
F32R = mybir.dt.float32r
BF16 = mybir.dt.bfloat16
ALU = mybir.AluOpType
ACT = mybir.ActivationFunctionType
AX_X = mybir.AxisListType.X

P = 128
BANK = 512
LN_EPS = 1e-5
ROUTED_SCALE = 2.5
NEG_INF = -1.0e9
Q_PARTS = (0, 0, 1, 1, 0, 2)
K_PARTS = (0, 1, 0, 1, 2, 0)


def build_layer(nc, x, wq, wk, wv, wo, wr, bias, wg, wu, wd, out):
    NB, SEQ, D = x.shape
    T = NB * SEQ
    NT = T // P
    KC = D // P
    KV = wk.shape[1]
    HD = 16
    NH = D // HD
    NG = KV // HD
    REP = NH // NG
    E, _, I = wg.shape
    EG, PG = 4, E // 4
    NBLK = T // BANK
    TB = BANK // P
    SCALE = float(HD) ** -0.5
    NPART = len(Q_PARTS)
    KROWS = NPART * HD
    NGRP = NB * NG
    KT = SEQ // P
    QB = SEQ // BANK
    STEPS = QB * KT
    UNITS = STEPS * REP
    PAIRS = REP * KT
    MX_STEPS = 14
    RING = 3
    WA = D + 2 * KV + E
    VR = KV + E
    WE = KC * I * 2 + D

    x_t = x.rearrange("b s d -> (b s) d").rearrange("(t p) d -> p t d", p=P)
    out_t = out.rearrange("b s d -> (b s) d").rearrange("(t p) d -> p t d", p=P)
    q_parts = nc.dram_tensor("q_parts", [3, NB * D, SEQ], BF16, kind="Internal").ap()
    k_parts = nc.dram_tensor("k_parts", [3, NB * KV, SEQ], BF16, kind="Internal").ap()
    attn_num = nc.dram_tensor("attn_num", [NB * D, SEQ], F32, kind="Internal").ap()
    attn_sum = nc.dram_tensor("attn_sum", [NB * NH, SEQ], F32, kind="Internal").ap()
    attn_inv = nc.dram_tensor("attn_inv", [NB * P, SEQ], F32, kind="Internal").ap()

    with ExitStack() as ctx:
        def sb(name, shape, dt, scope=ctx):
            return scope.enter_context(nc.sbuf_tensor(name, shape, dt))

        def sem(name):
            return ctx.enter_context(nc.semaphore(name))

        psum = ctx.enter_context(nc.psum_tensor("psum", [P, 8 * BANK], F32))
        banks = [psum[:, BANK * i:BANK * (i + 1)] for i in range(8)]

        X = sb("X", [P, NT, D], F32)
        xT_hi = sb("xT_hi", [P, KC, T], F32R)
        xT_lo = sb("xT_lo", [P, KC, T], F32R)
        V_all = sb("V_all", [P, NGRP, KT, HD], F32)
        logits = sb("logits", [P, NT, E], F32)
        scores = sb("scores", [P, NT, E], F32)
        combine = sb("combine", [P, NT, E], F32)
        ident = sb("ident", [P, P], F32)
        ident_bf = sb("ident_bf", [P, P], BF16)
        bias_sb = sb("bias_sb", [P, E], F32)
        earlier = sb("earlier", [P, EG, EG], F32)
        wo_hi = sb("wo_hi", [P, KC, D], F32R)
        wo_lo = sb("wo_lo", [P, KC, D], F32R)
        w_raw = [sb(f"w_raw{p}", [P, WE], F32) for p in range(2)]
        cnt = sb("cnt", [P, 3, NT], F32)

        sa = ExitStack()
        wa = sb("wa", [P, KC, WA], F32, sa)
        wa_hi = sb("wa_hi", [P, KC, WA], F32R, sa)
        wa_lo = sb("wa_lo", [P, KC, WA], F32R, sa)
        wo_sb = sb("wo_sb", [P, KC, D], F32, sa)
        xn = sb("xn", [P, TB, D], F32, sa)
        stats = sb("stats", [P, NT, 6], F32, sa)
        mv = sb("mv", [P, NT, 2], F32, sa)
        var_eps = sb("var_eps", [P, NT], F32, sa)
        std = sb("std", [P, NT], F32, sa)
        rstd0 = sb("rstd0", [P, NT], F32, sa)
        newton = sb("newton", [P, NT], F32, sa)
        rstd = sb("rstd", [P, NT], F32, sa)
        shift = sb("shift", [P, NT], F32, sa)
        part = [sb(f"part_{j}", [P, 3, BANK], BF16, sa) for j in range(3)]
        rest = [sb(f"rest_{j}", [P, BANK], F32, sa) for j in range(3)]
        sa.close()
        sc = ExitStack()
        num_sb = sb("num_sb", [P, 2, KC, BANK], F32, sc)
        inv_sb = sb("inv_sb", [P, 2, BANK], F32, sc)
        sums = sb("sums", [P, NB, SEQ * NH // P], F32, sc)
        inv = sb("inv", [P, NB, SEQ * NH // P], F32, sc)
        attn = sb("attn", [P, KC, BANK], F32, sc)
        attn_hi = sb("attn_hi", [P, KC, BANK], F32R, sc)
        attn_lo = sb("attn_lo", [P, KC, BANK], F32R, sc)
        sc.close()
        sa2 = ExitStack()
        hold = sb("hold", [P, 8240], F32, sa2)
        bb = ExitStack()
        QS = [sb("QS0", [P, REP, SEQ], BF16, bb)]
        KS = [sb(f"KS{p}", [P, SEQ], BF16, bb) for p in range(RING)]
        V = [sb(f"V{p}", [P, KT, 2 * HD], F32, bb) for p in range(RING)]
        probs = [sb(f"probs{p}", [P, REP, BANK], F32, bb) for p in range(2)]
        qmax = sb("qmax", [P, PAIRS], F32, bb)
        mrest = sb("mrest", [P, PAIRS], F32, bb)
        mparts = sb("mparts", [P, 3, PAIRS], BF16, bb)
        mrows = sb("mrows", [3 * PAIRS, P], BF16, bb)
        O_sb = sb("O_sb", [P, QB, BANK], F32, bb)
        b2 = ExitStack()
        QS += [sb(f"QS{p}", [P, REP, SEQ], BF16, b2) for p in range(1, RING)]
        b2.close()
        rt = ExitStack()
        choice = sb("choice", [P, NT, EG, PG], F32, rt)
        work1 = sb("work1", [P, NT, E], F32, rt)
        work2 = sb("work2", [P, NT, E], F32, rt)
        work3 = sb("work3", [P, NT, E], F32, rt)
        top8 = sb("top8", [P, NT, 8], F32, rt)
        gsc = sb("gsc", [P, NT, EG], F32, rt)
        small = sb("small", [P, 4, NT, EG], F32, rt)
        rt.close()
        bb.close()
        se = ExitStack()
        w_hi = [sb(f"w_hi{p}", [P, WE], F32R, se) for p in range(2)]
        w_lo = [sb(f"w_lo{p}", [P, WE], F32R, se) for p in range(2)]
        act_g = [sb(f"act_g{p}", [P, BANK], F32, se) for p in range(2)]
        h = [sb(f"h{p}", [P, BANK], F32, se) for p in range(2)]
        h_hi = [sb(f"h_hi{p}", [P, BANK], F32R, se) for p in range(2)]
        h_lo = [sb(f"h_lo{p}", [P, BANK], F32R, se) for p in range(2)]
        se.close()
        sa2.close()

        x_loaded = [sem(f"x_loaded{c}") for c in range(NBLK)]
        w_loaded = sem("w_loaded")
        consts = sem("consts")
        wa_hi_done, wa_lo_done = sem("wa_hi_done"), sem("wa_lo_done")
        ln_step = sem("ln_step")
        ve_done, std_done, rstd_done, xn_done = sem("ve_done"), sem("std_done"), sem("rstd_done"), sem("xn_done")
        tp_done, hi_done, lo_done = sem("tp_done"), sem("hi_done"), sem("lo_done")
        qk_done, vr_done, vr_read = sem("qk_done"), sem("vr_done"), sem("vr_read")
        p1_done, rest_done, p2_done, p3_done = sem("p1_done"), sem("rest_done"), sem("p2_done"), sem("p3_done")
        parts_stored = sem("parts_stored")
        stacks_loaded = [sem(f"stacks_loaded{p}") for p in range(RING)]
        v_loaded = [sem(f"v_loaded{p}") for p in range(RING)]
        negmax_loaded = sem("negmax_loaded")
        mx_done, mx_read = sem("mx_done"), sem("mx_read")
        chain = sem("chain")
        mparts_done, mT_done, mrows_done = sem("mparts_done"), sem("mT_done"), sem("mrows_done")
        st_done, exp_done, pv_done = sem("st_done"), sem("exp_done"), sem("pv_done")
        o_done, o_stored = sem("o_done"), sem("o_stored")
        scores_done, route = sem("scores_done"), sem("route")
        attn_loaded = [sem("attn_loaded0"), sem("attn_loaded1")]
        sums_loaded, inv_done, inv_stored = sem("sums_loaded"), sem("inv_done"), sem("inv_stored")
        attn_done, ahi_done, alo_done = sem("attn_done"), sem("ahi_done"), sem("alo_done")
        y_done, acc_done = sem("y_done"), sem("acc_done")
        we_loaded = [sem("we_loaded0"), sem("we_loaded1")]
        whi_done, wlo_done = sem("whi_done"), sem("wlo_done")
        g_done, u_done, silu_done = sem("g_done"), sem("u_done"), sem("silu_done")
        h_done, hhi_done, hlo_done = sem("h_done"), sem("hhi_done"), sem("hlo_done")
        stored = sem("stored")

        EXP0 = UNITS
        PV0 = 2
        O0 = 1

        def ring_before(u):
            if u >= 3:
                return u - 2
            return max(v for v in range(UNITS) if v % 3 == u) + 1 - UNITS

        def mx_pairs(step):
            s0, s1 = min(step, MX_STEPS), min(step + 1, MX_STEPS)
            return range(PAIRS * s0 // MX_STEPS, PAIRS * s1 // MX_STEPS)

        def turn(k):
            return k + (k + 1) // 2 if isinstance(k, int) and k < 2 * NBLK else k + NBLK

        def three(pe, psum, lhs, rhs):
            terms = [(l, r) for (lh, ll), (rh, rl) in zip(lhs, rhs) for l, r in ((lh, rh), (lh, rl), (ll, rh))]
            for i, (l, r) in enumerate(terms):
                last = pe.matmul(psum, l, r, start=(i == 0), stop=(i == len(terms) - 1))
            return last

        block = ctx.enter_context(nc.Block())

        @block.sync
        def _(sp):
            for c in range(NBLK):
                sp.dma_start(X[:, TB * c:TB * (c + 1), :], x_t[:, TB * c:TB * (c + 1), :]).then_inc(x_loaded[c], 16)
            def store_parts(n):
                for j in range(3):
                    M = P if j < 2 else KV
                    dst, row = (q_parts, D * (n // 2) + P * j) if j < 2 else (k_parts, KV * (n // 2))
                    for done in (p1_done, p2_done, p3_done):
                        sp.wait_ge(done, 3 * n + j + 1)
                    sp.dma_start(dst[:, row:row + M, BANK * (n % 2):BANK * (n % 2 + 1)].rearrange("i p t -> p i t"),
                                 part[j][0:M, :, :]).then_inc(parts_stored, 16)

            def load_stacks(m, p):
                for s, (i, j) in enumerate(zip(Q_PARTS, K_PARTS)):
                    sp.dma_start(QS[p][HD * s:HD * (s + 1), :, :],
                                 q_parts[i, bass.ds(m * (REP * HD), REP * HD), :].rearrange("(h d) t -> d h t", d=HD)
                                 ).then_inc(stacks_loaded[p], 16)
                    sp.dma_start(KS[p][HD * s:HD * (s + 1), :],
                                 k_parts[j, bass.ds(m * HD, HD), :]).then_inc(stacks_loaded[p], 16)

            def load_v(m, p):
                sp.dma_start(V[p][:, :, 0:HD], V_all[:, bass.ds(m, 1), :, :].rearrange("p m t d -> p (m t) d")
                             ).then_inc(v_loaded[p], 16)

            def negmax(m, p):
                sp.wait_ge(mrows_done, m + 1)
                sp.dma_start(QS[p][KROWS:KROWS + 3, :, :].rearrange("a h (t q) -> a (h t) q", q=P),
                             mrows[:, :]).then_inc(negmax_loaded, 16)

            def next_loads(n, p):
                sp.wait_ge(st_done, UNITS * n + UNITS)
                sp.wait_ge(parts_stored, 16 * 3 * NBLK)
                load_stacks(n + RING, p)
                sp.wait_ge(pv_done, STEPS * n + STEPS + PV0)
                sp.wait_ge(vr_read, 2 * NBLK)
                load_v(n + RING, p)

            for n in range(NBLK):
                store_parts(n)
                if n == 3:
                    sp.wait_ge(parts_stored, 16 * 3 * 2)
                    sp.wait_ge(vr_read, 2 * 2)
                    load_stacks(0, 0)
                    load_v(0, 0)
            for p in range(1, RING):
                load_stacks(p, p)
                load_v(p, p)
            negmax(0, 0)
            with sp.Fori(0, NGRP // RING - 1) as i:
                for p in range(RING):
                    negmax(RING * i + p + 1, (p + 1) % RING)
                    next_loads(RING * i + p, p)
            for n in range(NGRP - 1 - RING, NGRP - 1):
                negmax(n + 1, (n + 1) % RING)
                if n + RING < NGRP:
                    next_loads(n, n % RING)

            num_v = attn_num.rearrange("(b k p) t -> b p k t", p=P, k=KC)
            inv_v = attn_inv.rearrange("(b p) t -> b p t", p=P)
            sum_c = attn_sum.rearrange("(b h) (s c) -> (h s) b c", b=NB, c=P)
            inv_c = attn_inv.rearrange("(b d h) (s c) -> b (h s) d c", b=NB, h=NH, c=P)

            def load_sums(b0, b1):
                sp.wait_ge(o_stored, 16 * 2 * REP * NG * b1)
                sp.dma_start(sums[:, b0:b1, :], sum_c[:, b0:b1, :]).then_inc(sums_loaded, 16)

            def store_inverses(b0, b1, count):
                sp.wait_ge(inv_done, count)
                for b in range(b0, b1):
                    sp.dma_start(inv_c[b], inv[:, b, :].unsqueeze(1).broadcast_to([P, HD // KC, P])).then_inc(inv_stored, 16)
                sp.wait_ge(inv_stored, 16 * b1)

            def load_attn(n):
                b, cols = n // 2, slice(BANK * (n % 2), BANK * (n % 2 + 1))
                sp.dma_start(num_sb[:, n % 2, :, :], num_v[b, :, :, cols]).then_inc(attn_loaded[n % 2], 16)
                sp.dma_start(inv_sb[:, n % 2, :], inv_v[b, :, cols]).then_inc(attn_loaded[n % 2], 16)

            def load_expert(e, p):
                w = w_raw[p]
                sp.dma_start(w[:, 0:KC * I].rearrange("p (k i) -> p k i", k=KC),
                             wg[bass.ds(e, 1), :, :].rearrange("e (k p) i -> p (e k) i", p=P)).then_inc(we_loaded[p], 16)
                sp.dma_start(w[:, KC * I:2 * KC * I].rearrange("p (k i) -> p k i", k=KC),
                             wu[bass.ds(e, 1), :, :].rearrange("e (k p) i -> p (e k) i", p=P)).then_inc(we_loaded[p], 16)
                sp.dma_start(w[:, 2 * KC * I:WE],
                             wd[bass.ds(e, 1), :, :].rearrange("e i d -> i (e d)")).then_inc(we_loaded[p], 16)

            load_expert(0, 0)
            load_expert(1, 1)
            load_sums(0, NB - 1)
            store_inverses(0, NB - 1, 1)
            load_attn(0)
            load_attn(1)
            load_sums(NB - 1, NB)

            def refill(e, p):
                sp.wait_ge(whi_done, e - 1)
                sp.wait_ge(wlo_done, e - 1)
                load_expert(e, p)

            for n in range(2, NBLK):
                sp.wait_ge(attn_done, n - 1)
                load_attn(n)
                if n <= 3:
                    refill(n, n - 2)
                if n == 3:
                    store_inverses(NB - 1, NB, 2)
            with sp.Fori(2, E // 2) as i:
                for p in range(2):
                    refill(2 * i + p, p)
            for n in range(NBLK):
                sp.wait_ge(acc_done, TB * (turn((E - 1) * NBLK + n) + 1))
                sp.dma_start(out_t[:, TB * n:TB * (n + 1), :], X[:, TB * n:TB * (n + 1), :]).then_inc(stored, 16)
            sp.wait_ge(stored, 16 * NBLK)

        @block.gpsimd
        def _(pool):
            pool.memset(ident[:, :], 0.0).then_inc(consts, 1)
            pool.memset(earlier[:, :, :], 1.0).then_inc(consts, 1)
            for p in range(RING):
                pool.memset(V[p][:, :, HD:2 * HD], 1.0).then_inc(v_loaded[p], 16)
            pool.wait_ge(consts, 2)
            pool.affine_select(out=ident[:, :], in_=ident[:, :], compare_op=ALU.not_equal, fill=1.0, base=0,
                               pattern=[[-1, P]], channel_multiplier=1).then_inc(consts, 1)
            pool.affine_select(out=earlier[:, :, :], in_=earlier[:, :, :], compare_op=ALU.is_gt, fill=0.0, base=0,
                               pattern=[[1, EG], [-1, EG]], channel_multiplier=0).then_inc(consts, 1)
            for n in range(NBLK):
                for j in range(3):
                    M = P if j < 2 else KV
                    u = 3 * n + j
                    if n >= 1:
                        pool.wait_ge(parts_stored, 16 * 3 * n)
                    pool.wait_ge(p2_done, u + 1)
                    pool.wait_ge(rest_done, u + 1)
                    pool.tensor_tensor(part[j][0:M, 2, :], rest[j][0:M, :], part[j][0:M, 1, :],
                                       ALU.subtract).then_inc(p3_done, 1)
            num_h = attn_num.rearrange("(b d h) t -> b h d t", b=NB, h=NH)
            with pool.Fori(0, NB) as b:
                for g in range(NG):
                    n = b * NG + g
                    pool.wait_ge(o_done, 2 * n + 2 + O0)
                    for r in range(REP):
                        at = 2 * HD * r
                        pool.dma_start(num_h[bass.ds(b, 1), REP * g + r, :, :].rearrange("a d t -> (a d) t"),
                                       O_sb[at:at + HD, :, :]).then_inc(o_stored, 16)
                        pool.dma_start(attn_sum[bass.ds(n * REP + r, 1), :],
                                       O_sb[at + HD:at + HD + 1, :, :]).then_inc(o_stored, 16)

            for n in range(NBLK):
                pool.wait_ge(attn_loaded[n % 2], 32 * (n // 2 + 1))
                if n >= 1:
                    pool.wait_ge(ahi_done, n)
                    pool.wait_ge(alo_done, n)
                pool.tensor_tensor(attn[:, :, :], num_sb[:, n % 2, :, :],
                                   inv_sb[:, n % 2, :].unsqueeze(1).broadcast_to([P, KC, BANK]), ALU.mult).then_inc(attn_done, 1)

        @block.scalar
        def _(act):
            act.dma_start(wa[:, :, 0:D], wq.rearrange("(k p) n -> p k n", p=P)).then_inc(w_loaded, 16)
            act.dma_start(wa[:, :, D:D + KV], wk.rearrange("(k p) n -> p k n", p=P)).then_inc(w_loaded, 16)
            act.dma_start(wa[:, :, D + KV:D + 2 * KV], wv.rearrange("(k p) n -> p k n", p=P)).then_inc(w_loaded, 16)
            act.dma_start(wa[:, :, D + 2 * KV:WA], wr.rearrange("(k p) n -> p k n", p=P)).then_inc(w_loaded, 16)
            act.dma_start(wo_sb[:, :, :], wo.rearrange("d h n -> (d h) n").rearrange("(k p) n -> p k n", p=P)).then_inc(w_loaded, 16)
            act.dma_start(bias_sb[:, :], bias.rearrange("(a n) -> a n", a=1).broadcast_to([P, E])).then_inc(w_loaded, 16)

            def root(c):
                act.wait_ge(ve_done, c + 1)
                act.activation(std[:, TB * c:TB * (c + 1)], var_eps[:, TB * c:TB * (c + 1)], ACT.Sqrt).then_inc(std_done, 1)

            def normalise(c):
                act.wait_ge(rstd_done, c + 1)
                for i in range(TB):
                    t = TB * c + i
                    if c >= 1:
                        act.wait_ge(tp_done, 2 * (c - 1) + i // 2 + 1)
                    act.activation(xn[:, i, :], X[:, t, :], ACT.Identity, bias=shift[:, t:t + 1],
                                   scale=rstd[:, t:t + 1]).then_inc(xn_done, 1)

            def hi_of_x(c):
                for q in range(2 * c, 2 * c + 2):
                    act.wait_ge(tp_done, q + 1)
                    act.activation(xT_hi[:, :, 2 * P * q:2 * P * (q + 1)],
                                   banks[q % 2].rearrange("p (k t) -> p k t", k=KC), ACT.Copy).then_inc(hi_done, 1)

            root(0)
            root(1)
            root(2)
            normalise(0)
            act.wait_ge(w_loaded, 96)
            act.activation(wa_hi[:, :, :], wa[:, :, :], ACT.Copy).then_inc(wa_hi_done, 1)
            hi_of_x(0)
            normalise(1)
            act.activation(wo_hi[:, :, :], wo_sb[:, :, :], ACT.Copy).then_inc(wa_hi_done, 1)
            for c in range(NBLK):
                if c >= 1:
                    act.wait_ge(parts_stored, 16 * 3 * c)
                for j in range(3):
                    M = P if j < 2 else KV
                    act.wait_ge(qk_done, 3 * c + j + 1)
                    act.activation(part[j][0:M, 0, :], banks[2 + j][0:M, :], ACT.Copy).then_inc(p1_done, 1)
                if c + 1 < NBLK:
                    hi_of_x(c + 1)
                for j in range(3):
                    M = P if j < 2 else KV
                    act.wait_ge(rest_done, 3 * c + j + 1)
                    act.activation(part[j][0:M, 1, :], rest[j][0:M, :], ACT.Copy).then_inc(p2_done, 1)
                if c + 2 < NBLK:
                    normalise(c + 2)
                if c + 3 < NBLK:
                    root(c + 3)
                act.wait_ge(vr_done, c + 1)
                vr = banks[5 + c % 2][:, 0:TB * VR].rearrange("p (t n) -> p t n", t=TB)
                act.activation(V_all[:, NG * (c // 2):NG * (c // 2 + 1), TB * (c % 2):TB * (c % 2 + 1), :].rearrange("p g t d -> p t g d"),
                               vr[:, :, 0:KV].rearrange("p t (g d) -> p t g d", d=HD), ACT.Copy).then_inc(vr_read, 1)
                act.activation(logits[:, TB * c:TB * (c + 1), :], vr[:, :, KV:VR], ACT.Copy).then_inc(vr_read, 1)
            act.wait_ge(vr_read, 2 * NBLK)
            act.activation(scores[:, :, :], logits[:, :, :], ACT.Sigmoid).then_inc(scores_done, 1)

            def exps(n):
                for s in range(STEPS):
                    for r in range(REP):
                        u = REP * s + r
                        if r == 0:
                            act.wait_ge(pv_done, STEPS * n + s - 1 + PV0)
                        act.wait_ge(st_done, UNITS * n + u + 1)
                        act.activation(probs[s % 2][:, r, :], banks[u % 3][:, :], ACT.Exp, scale=SCALE).then_inc(exp_done, 1)

            with act.Fori(0, NGRP) as n:
                exps(n)

            def hi_of_attn(n):
                act.wait_ge(attn_done, n + 1)
                if n >= 1:
                    act.wait_ge(y_done, 2 * turn(2 * n - 2) + 4)
                act.activation(attn_hi[:, :, :], attn[:, :, :], ACT.Copy).then_inc(ahi_done, 1)

            def w_split(p, loads):
                act.wait_ge(we_loaded[p], loads)
                act.activation(w_hi[p][:, :], w_raw[p][:, :], ACT.Copy).then_inc(whi_done, 1)

            def silu(k, par, first=False):
                act.wait_ge(g_done, k + 1)
                if not first:
                    act.wait_ge(h_done, k - 1)
                act.activation(act_g[par][:, :], banks[par][:, :], ACT.Silu).then_inc(silu_done, 1)

            def hi_of_h(k, par, first=False):
                act.wait_ge(h_done, k + 1)
                if not first:
                    act.wait_ge(y_done, 2 * turn(k - 2) + 2)
                act.activation(h_hi[par][:, :], h[par][:, :], ACT.Copy).then_inc(hhi_done, 1)

            act.wait_ge(pv_done, STEPS * NGRP + PV0)
            w_split(0, 48)
            silu(0, 0, True)
            hi_of_h(0, 0, True)

            def expert_pair(i, last=False, first=False):
                for p in range(2):
                    for j in range(NBLK):
                        k = 2 * NBLK * i + NBLK * p + j
                        final = last and p == 1
                        if j == 1 and not final:
                            act.wait_ge(y_done, 2 * turn(max(k - 2, 0) if first else k - 2) + 2)
                            w_split(1 - p, 48 * i + 48 * p + 48)
                        if not (final and j == NBLK - 1):
                            silu(k + 1, (j + 1) % 2, first and k == 0)
                            hi_of_h(k + 1, (j + 1) % 2, first and k == 0)
                        if first and j % 2 == 0:
                            hi_of_attn(k // 2)

            expert_pair(0, first=True)
            with act.Fori(1, E // 2 - 1) as i:
                expert_pair(i)
            expert_pair(E // 2 - 1, last=True)

        @block.vector
        def _(dve):
            dve.memset(KS[0][KROWS:P, :], 1.0).then_inc(exp_done, EXP0)
            dve.memset(KS[1][KROWS:P, :], 1.0).then_inc(pv_done, PV0)
            dve.memset(KS[2][KROWS:P, :], 1.0).then_inc(o_done, O0)
            step = [0]

            def link(ins, s=ln_step):
                ins.then_inc(s, 1)
                step[0] += 1
                dve.wait_ge(s, step[0])

            def ln_stats(c):
                tiles = range(TB * c, TB * (c + 1))
                sl = slice(TB * c, TB * (c + 1))
                dve.wait_ge(x_loaded[c], 16)
                for t in tiles:
                    last = dve.bn_stats(stats[:, t, :], X[:, t, :])
                link(last)
                for t in tiles:
                    last = dve.bn_aggr(mv[:, t, :], stats[:, t, :])
                link(last)
                dve.tensor_scalar(var_eps[:, sl], mv[:, sl, 1], LN_EPS, None, ALU.add).then_inc(ve_done, 1)

            def ln_scale(c):
                sl = slice(TB * c, TB * (c + 1))
                dve.wait_ge(std_done, c + 1)
                dve.wait_ge(ve_done, c + 1)
                link(dve.reciprocal(rstd0[:, sl], std[:, sl]))
                link(dve.tensor_tensor(newton[:, sl], rstd0[:, sl], rstd0[:, sl], ALU.mult))
                link(dve.tensor_tensor(newton[:, sl], newton[:, sl], var_eps[:, sl], ALU.mult))
                link(dve.tensor_scalar(newton[:, sl], newton[:, sl], -0.5, 1.5, ALU.mult, ALU.add))
                link(dve.tensor_tensor(rstd[:, sl], rstd0[:, sl], newton[:, sl], ALU.mult))
                dve.scalar_tensor_tensor(out=shift[:, sl], in0=mv[:, sl, 0], scalar=-1.0, in1=rstd[:, sl],
                                         op0=ALU.mult, op1=ALU.mult).then_inc(rstd_done, 1)

            ln_stats(0)
            dve.wait_ge(consts, 4)
            dve.tensor_copy(ident_bf[:, :], ident[:, :]).then_inc(consts, 1)
            ln_stats(1)
            ln_scale(0)
            ln_stats(2)
            ln_scale(1)

            def lo_of_x(c):
                for q in range(2 * c, 2 * c + 2):
                    dve.wait_ge(hi_done, q + 1)
                    cols = slice(2 * P * q, 2 * P * (q + 1))
                    dve.tensor_tensor(xT_lo[:, :, cols], banks[q % 2].rearrange("p (k t) -> p k t", k=KC),
                                      xT_hi[:, :, cols].bitcast(F32), ALU.subtract).then_inc(lo_done, 1)

            dve.wait_ge(wa_hi_done, 1)
            dve.tensor_tensor(wa_lo[:, :, :], wa[:, :, :], wa_hi[:, :, :].bitcast(F32), ALU.subtract).then_inc(wa_lo_done, 1)
            lo_of_x(0)
            dve.wait_ge(wa_hi_done, 2)
            dve.tensor_tensor(wo_lo[:, :, :], wo_sb[:, :, :], wo_hi[:, :, :].bitcast(F32), ALU.subtract).then_inc(wa_lo_done, 1)
            for c in range(NBLK):
                for j in range(3):
                    M = P if j < 2 else KV
                    u = 3 * c + j
                    dve.wait_ge(p1_done, u + 1)
                    if c >= 1:
                        dve.wait_ge(p3_done, u - 2)
                    dve.tensor_tensor(rest[j][0:M, :], banks[2 + j][0:M, :], part[j][0:M, 0, :],
                                      ALU.subtract).then_inc(rest_done, 1)
                if c + 1 < NBLK:
                    lo_of_x(c + 1)
                if c + 2 < NBLK:
                    ln_scale(c + 2)
                if c + 3 < NBLK:
                    ln_stats(c + 3)

            def maxima(m, between=None):
                for v in range(PAIRS):
                    dve.wait_ge(mx_done, PAIRS * m + v + 1)
                    at = BANK * (3 + 2 * (v % 2))
                    dve.tensor_reduce(qmax[:, v:v + 1], psum[:, at:at + 2 * BANK], AX_X, ALU.max).then_inc(mx_read, 1)
                    if between is not None and v == mx_pairs(KT)[-1]:
                        output(between, 0)
                dve.wait_ge(mx_read, PAIRS * m + PAIRS)
                dve.tensor_scalar(mparts[:, 0, :], qmax[:, :], -1.0, None, ALU.mult).then_inc(chain, 1)
                dve.wait_ge(chain, 3 * m + 1)
                dve.scalar_tensor_tensor(out=mrest[:, :], in0=qmax[:, :], scalar=-1.0, in1=mparts[:, 0, :],
                                         op0=ALU.mult, op1=ALU.subtract).then_inc(chain, 1)
                dve.wait_ge(chain, 3 * m + 2)
                dve.tensor_copy(mparts[:, 1, :], mrest[:, :]).then_inc(chain, 1)
                dve.wait_ge(chain, 3 * m + 3)
                dve.tensor_tensor(mparts[:, 2, :], mrest[:, :], mparts[:, 1, :], ALU.subtract).then_inc(mparts_done, 1)
                dve.wait_ge(mT_done, m + 1)
                dve.wait_ge(negmax_loaded, 16 * m)
                dve.tensor_copy(mrows[:, :], banks[3][0:3 * PAIRS, 0:P // 2].bitcast(BF16)).then_inc(mrows_done, 1)

            def output(n, qb):
                dve.wait_ge(pv_done, STEPS * n + KT * (qb + 1) + PV0)
                if not isinstance(n, int) or n > 0:
                    dve.wait_ge(o_stored, 16 * 2 * REP * n)
                dve.tensor_copy(O_sb[:, qb, :], banks[7]).then_inc(o_done, 1)

            maxima(0)
            maxima(1, 0)
            output(0, 1)
            with dve.Fori(1, NGRP - 1) as n:
                maxima(n + 1, n)
                output(n, 1)

            step[0] = 0
            r_ = lambda ins: link(ins, route)
            dve.wait_ge(scores_done, 1)
            dve.wait_ge(st_done, UNITS * (NGRP - 1))
            sc4 = scores[:, :, :].rearrange("p t (g e) -> p t g e", g=EG)
            b4 = bias_sb[:, :].rearrange("p (a g e) -> p a g e", a=1, g=EG).broadcast_to([P, NT, EG, PG])
            r_(dve.tensor_tensor(choice[:, :, :, :], sc4, b4, ALU.add))
            c_lo, c_hi = choice[:, :, :, 0:PG:2], choice[:, :, :, 1:PG:2]
            pair_max = work1[:, :, 0:2 * EG].rearrange("p t (g e) -> p t g e", g=EG)
            pair_min = work2[:, :, 0:2 * EG].rearrange("p t (g e) -> p t g e", g=EG)
            r_(dve.tensor_tensor(pair_max, c_lo, c_hi, ALU.max))
            r_(dve.tensor_tensor(pair_min, c_lo, c_hi, ALU.min))
            first, second, third = small[:, 0, :, :], small[:, 1, :, :], small[:, 2, :, :]
            r_(dve.tensor_tensor(first, pair_max[:, :, :, 0], pair_max[:, :, :, 1], ALU.max))
            r_(dve.tensor_tensor(second, pair_max[:, :, :, 0], pair_max[:, :, :, 1], ALU.min))
            r_(dve.tensor_tensor(third, pair_min[:, :, :, 0], pair_min[:, :, :, 1], ALU.max))
            r_(dve.tensor_tensor(second, second, third, ALU.max))
            r_(dve.tensor_tensor(gsc[:, :, :], first, second, ALU.add))
            other = gsc[:, :, :].unsqueeze(2).broadcast_to([P, NT, EG, EG])
            own = gsc[:, :, :].unsqueeze(3).broadcast_to([P, NT, EG, EG])
            more = work1[:, :, :].rearrange("p t (g e) -> p t g e", g=EG)
            same = work2[:, :, :].rearrange("p t (g e) -> p t g e", g=EG)
            lower = earlier[:, :, :].unsqueeze(1).broadcast_to([P, NT, EG, EG])
            r_(dve.tensor_tensor(more, other, own, ALU.is_gt))
            r_(dve.tensor_tensor(same, other, own, ALU.is_equal))
            r_(dve.tensor_tensor(same, same, lower, ALU.mult))
            r_(dve.tensor_tensor(more, more, same, ALU.add))
            rank, keep, drop = small[:, 0, :, :], small[:, 1, :, :], small[:, 2, :, :]
            r_(dve.tensor_reduce(rank, more, AX_X, ALU.add))
            r_(dve.tensor_scalar(keep, rank, 2.0, None, ALU.is_lt))
            r_(dve.tensor_scalar(drop, keep, -NEG_INF, NEG_INF, ALU.mult, ALU.add))
            wide = lambda a: a.unsqueeze(3).broadcast_to([P, NT, EG, PG])
            r_(dve.tensor_tensor(choice[:, :, :, :], choice[:, :, :, :], wide(keep), ALU.mult))
            r_(dve.tensor_tensor(choice[:, :, :, :], choice[:, :, :, :], wide(drop), ALU.add))
            masked = choice[:, :, :, :].rearrange("p t g e -> p t (g e)")
            for t in range(NT):
                last = dve.max(top8[:, t, :], masked[:, t, :])
            r_(last)
            fourth = top8[:, :, 3:4].broadcast_to([P, NT, E])
            above, equal, run = work1[:, :, :], work2[:, :, :], work3[:, :, :]
            r_(dve.tensor_tensor(above, masked, fourth, ALU.is_gt))
            r_(dve.tensor_tensor(equal, masked, fourth, ALU.is_equal))
            r_(dve.tensor_reduce(cnt[:, 0, :], above, AX_X, ALU.add))
            r_(dve.tensor_scalar(cnt[:, 1, :], cnt[:, 0, :], -1.0, 4.0, ALU.mult, ALU.add))
            src, dst = equal, run
            for d in (1, 2, 4, 8):
                r_(dve.tensor_copy(dst[:, :, 0:d], src[:, :, 0:d]))
                r_(dve.tensor_tensor(dst[:, :, d:E], src[:, :, d:E], src[:, :, 0:E - d], ALU.add))
                if d == 1:
                    src, dst = run, combine[:, :, :]
                else:
                    src, dst = dst, src
            counted, free = src, dst
            r_(dve.tensor_tensor(free, counted, cnt[:, 1, :].unsqueeze(2).broadcast_to([P, NT, E]), ALU.is_le))
            r_(dve.tensor_tensor(free, free, equal, ALU.mult))
            r_(dve.tensor_tensor(above, above, free, ALU.add))
            r_(dve.tensor_tensor(above, above, scores[:, :, :], ALU.mult))
            r_(dve.tensor_reduce(cnt[:, 0, :], above, AX_X, ALU.add))
            r_(dve.tensor_scalar(cnt[:, 0, :], cnt[:, 0, :], 1e-20, None, ALU.add))
            r_(dve.reciprocal(cnt[:, 2, :], cnt[:, 0, :]))
            r_(dve.tensor_scalar(cnt[:, 2, :], cnt[:, 2, :], ROUTED_SCALE, None, ALU.mult))
            r_(dve.tensor_tensor(combine[:, :, :], above, cnt[:, 2, :].unsqueeze(2).broadcast_to([P, NT, E]), ALU.mult))
            output(NGRP - 1, 0)

            def inverses(b0, b1, count):
                dve.wait_ge(sums_loaded, 16 * count)
                dve.reciprocal(inv[:, b0:b1, :], sums[:, b0:b1, :]).then_inc(inv_done, 1)

            inverses(0, NB - 1, 1)
            output(NGRP - 1, 1)

            def lo_of_attn(n):
                dve.wait_ge(ahi_done, n + 1)
                if n >= 1:
                    dve.wait_ge(y_done, 2 * turn(2 * n - 2) + 4)
                dve.tensor_tensor(attn_lo[:, :, :], attn[:, :, :], attn_hi[:, :, :].bitcast(F32), ALU.subtract).then_inc(alo_done, 1)

            def y(turns, t):
                return banks[4 + 2 * (turns % 2) + t // 2][:, D * (t % 2):D * (t % 2 + 1)]

            added = {}

            def add_attn(n):
                r = turn(2 * n) + 1
                for t in range(TB):
                    dve.wait_ge(y_done, 2 * r + t // 2 + 1)
                    if n in added:
                        dve.wait_ge(acc_done, TB * added[n] + t + 1)
                    xt = X[:, TB * n + t, :]
                    dve.tensor_tensor(xt, y(r, t), xt, ALU.add).then_inc(acc_done, 1)
                added[n] = r

            def w_split(p, count):
                dve.wait_ge(whi_done, count)
                dve.tensor_tensor(w_lo[p][:, :], w_raw[p][:, :], w_hi[p][:, :].bitcast(F32), ALU.subtract).then_inc(wlo_done, 1)

            def gated(k, par, first=False):
                dve.wait_ge(u_done, k + 1)
                dve.wait_ge(silu_done, k + 1)
                if not first:
                    dve.wait_ge(hhi_done, k - 1)
                    dve.wait_ge(hlo_done, k - 1)
                dve.tensor_tensor(h[par][:, :], banks[2 + par][:, :], act_g[par][:, :], ALU.mult).then_inc(h_done, 1)
                dve.wait_ge(hhi_done, k + 1)
                dve.tensor_tensor(h_lo[par][:, :], h[par][:, :], h_hi[par][:, :].bitcast(F32), ALU.subtract).then_inc(hlo_done, 1)

            def add_expert(k, j, e):
                r = turn(k)
                for t in range(TB):
                    dve.wait_ge(y_done, 2 * r + t // 2 + 1)
                    if not isinstance(k, int):
                        dve.wait_ge(acc_done, TB * r + t - TB)
                    elif j in added:
                        dve.wait_ge(acc_done, TB * added[j] + t + 1)
                    tile = TB * j + t
                    dve.scalar_tensor_tensor(out=X[:, tile, :], in0=y(r if isinstance(r, int) else j, t),
                                             scalar=combine[:, tile, bass.ds(e, 1)], in1=X[:, tile, :],
                                             op0=ALU.mult, op1=ALU.add).then_inc(acc_done, 1)
                if isinstance(r, int):
                    added[j] = r

            w_split(0, 1)
            gated(0, 0, True)

            def expert_pair(i, last=False, first=False):
                for p in range(2):
                    for j in range(NBLK):
                        k = 2 * NBLK * i + NBLK * p + j
                        final = last and p == 1
                        if j == 1 and not final:
                            w_split(1 - p, 2 * i + p + 2)
                        if not (final and j == NBLK - 1):
                            gated(k + 1, (j + 1) % 2, first and k == 0)
                        if first and j % 2 == 0:
                            lo_of_attn(k // 2)
                        add_expert(k, j, 2 * i + p)
                        if first and j % 2 == 0:
                            add_attn(k // 2)
                        if first and k == 3:
                            inverses(NB - 1, NB, 2)

            expert_pair(0, first=True)
            added.clear()
            with dve.Fori(1, E // 2 - 1) as i:
                expert_pair(i)
            for j in range(NBLK):
                added[j] = turn((E - 3) * NBLK + j)
            expert_pair(E // 2 - 1, last=True)

        @block.tensor
        def _(pe):
            def transposes(c):
                for q in range(2 * c, 2 * c + 2):
                    if q >= 2:
                        pe.wait_ge(lo_done, q - 1)
                    for t in range(2):
                        pe.wait_ge(xn_done, 2 * q + t + 1)
                        for k in range(KC):
                            at = 2 * P * k + P * t
                            last = pe.transpose(banks[q % 2][:, at:at + P], xn[:, (2 * q + t) % TB, P * k:P * (k + 1)], ident[:, :])
                    last.then_inc(tp_done, 1)

            def xT(k, sl):
                return xT_hi[:, k, sl], xT_lo[:, k, sl]

            def project(c):
                sl = slice(BANK * c, BANK * (c + 1))
                pe.wait_ge(lo_done, 2 * c + 2)
                if c == 0:
                    pe.wait_ge(wa_lo_done, 1)
                for j in range(3):
                    if c >= 1:
                        pe.wait_ge(rest_done, 3 * (c - 1) + j + 1)
                    M = P if j < 2 else KV
                    lhs = [(wa_hi[:, k, P * j:P * j + M], wa_lo[:, k, P * j:P * j + M]) for k in range(KC)]
                    three(pe, banks[2 + j][0:M, :], lhs, [xT(k, sl) for k in range(KC)]).then_inc(qk_done, 1)

            def project_by_token(c):
                if c >= 2:
                    pe.wait_ge(vr_read, 2 * (c - 1))
                for t in range(TB):
                    at = BANK * c + P * t
                    rhs = [(wa_hi[:, k, D + KV:WA], wa_lo[:, k, D + KV:WA]) for k in range(KC)]
                    last = three(pe, banks[5 + c % 2][:, VR * t:VR * (t + 1)], [xT(k, slice(at, at + P)) for k in range(KC)], rhs)
                last.then_inc(vr_done, 1)

            pe.wait_ge(consts, 5)
            transposes(0)
            for c in range(NBLK):
                project(c)
                if c + 1 < NBLK:
                    transposes(c + 1)
                project_by_token(c)

            def max_pair(m, p, v):
                head, qt = v // KT, v % KT
                if not isinstance(m, int) or m > 0 or v >= 2:
                    pe.wait_ge(mx_read, PAIRS * m + v - 1)
                    if v == 0:
                        pe.wait_ge(mrows_done, m)
                for half in range(2):
                    last = pe.matmul(banks[3 + 2 * (v % 2) + half], QS[p][0:KROWS, head, P * qt:P * (qt + 1)],
                                     KS[p][0:KROWS, BANK * half:BANK * (half + 1)], start=True, stop=True)
                last.then_inc(mx_done, 1)

            def turn_maxima(m):
                pe.wait_ge(mparts_done, m + 1)
                pe.transpose(banks[3][0:3 * PAIRS, 0:P // 2].bitcast(BF16),
                             mparts[:, :, :].rearrange("p a q -> p (a q)"), ident_bf[:, :]).then_inc(mT_done, 1)

            def values(n, i, p, s):
                kt = s % KT
                pe.wait_ge(exp_done, UNITS * n + REP * (s + 1) + EXP0)
                if kt == 0:
                    pe.wait_ge(o_done, 2 * n + s // KT + O0)
                if s == 0:
                    pe.wait_ge(v_loaded[p], 16 * i + 32)
                for r in range(REP):
                    last = pe.matmul(banks[7][2 * HD * r:2 * HD * (r + 1), :], V[p][:, kt, :], probs[s % 2][:, r, :],
                                     start=(kt == 0), stop=(kt == KT - 1))
                last.then_inc(pv_done, 1)

            def attend(n, i, p, more=True):
                p1, i1 = (p + 1) % RING, i + (p + 1) // RING
                if more:
                    pe.wait_ge(stacks_loaded[p1], 16 * 2 * NPART * i1 + 16 * 2 * NPART)
                pe.wait_ge(negmax_loaded, 16 * n + 16)
                for s in range(STEPS):
                    qb, kt = s // KT, s % KT
                    mx = list(mx_pairs(s)) if more else []
                    for r in range(REP):
                        u = REP * s + r
                        pe.wait_ge(exp_done, UNITS * n + ring_before(u) + EXP0)
                        pe.matmul(banks[u % 3], KS[p][0:KROWS + 3, P * kt:P * (kt + 1)],
                                  QS[p][0:KROWS + 3, r, BANK * qb:BANK * (qb + 1)], start=True, stop=True).then_inc(st_done, 1)
                        if mx and r >= 1:
                            max_pair(n + 1, p1, mx.pop(0))
                        if r == 2 and s > 0:
                            values(n, i, p, s - 1)
                    if more and s == STEPS - 2:
                        turn_maxima(n + 1)
                values(n, i, p, STEPS - 1)

            pe.wait_ge(stacks_loaded[0], 16 * 2 * NPART)
            pe.wait_ge(rest_done, 3 * NBLK)
            pe.wait_ge(vr_read, 2 * NBLK)
            for v in range(PAIRS):
                max_pair(0, 0, v)
            turn_maxima(0)
            with pe.Fori(0, NGRP // RING) as i:
                for p in range(RING):
                    attend(RING * i + p, i, p)
            attend(NGRP - 1, NGRP // RING, 0, False)

            def project_attn(n):
                if n == 0:
                    pe.wait_ge(wa_lo_done, 2)
                pe.wait_ge(alo_done, n + 1)
                r = turn(2 * n) + 1
                for t in range(TB):
                    if r >= 2 and t % 2 == 0:
                        pe.wait_ge(acc_done, TB * (r - 2) + t + 2)
                    lhs = [(attn_hi[:, k, P * t:P * (t + 1)], attn_lo[:, k, P * t:P * (t + 1)]) for k in range(KC)]
                    rhs = [(wo_hi[:, k, :], wo_lo[:, k, :]) for k in range(KC)]
                    last = three(pe, banks[4 + 2 * (r % 2) + t // 2][:, D * (t % 2):D * (t % 2 + 1)], lhs, rhs)
                    if t % 2:
                        last.then_inc(y_done, 1)

            def gate_up(k, blk, p, par, first=False):
                sl = slice(BANK * blk, BANK * (blk + 1))
                rhs = [xT(c, sl) for c in range(KC)]
                for m, (read, done) in enumerate(((silu_done, g_done), (h_done, u_done))):
                    if not first:
                        pe.wait_ge(read, k - 1)
                    at = KC * I * m
                    lhs = [(w_hi[p][:, at + I * c:at + I * (c + 1)], w_lo[p][:, at + I * c:at + I * (c + 1)]) for c in range(KC)]
                    three(pe, banks[2 * m + par][:, :], lhs, rhs).then_inc(done, 1)

            def down(k, j, p):
                pe.wait_ge(hlo_done, k + 1)
                r = turn(k)
                for t in range(TB):
                    if t % 2 == 0 and not (isinstance(r, int) and r < 2):
                        pe.wait_ge(acc_done, TB * r - 2 * TB + t + 2)
                    sl = slice(P * t, P * (t + 1))
                    at = 2 * KC * I
                    par = r % 2 if isinstance(r, int) else j % 2
                    last = three(pe, banks[4 + 2 * par + t // 2][:, D * (t % 2):D * (t % 2 + 1)],
                                 [(h_hi[j % 2][:, sl], h_lo[j % 2][:, sl])], [(w_hi[p][:, at:WE], w_lo[p][:, at:WE])])
                    if t % 2:
                        last.then_inc(y_done, 1)

            pe.wait_ge(o_done, 2 * NGRP + O0)
            pe.wait_ge(wlo_done, 1)
            gate_up(0, 0, 0, 0, True)

            def expert_pair(i, last=False, first=False):
                for p in range(2):
                    for j in range(NBLK):
                        k = 2 * NBLK * i + NBLK * p + j
                        final = last and p == 1
                        if not (final and j == NBLK - 1):
                            if j == NBLK - 1:
                                pe.wait_ge(wlo_done, 2 * i + p + 2)
                                gate_up(k + 1, 0, 1 - p, 0)
                            else:
                                gate_up(k + 1, j + 1, p, (j + 1) % 2, first and k == 0)
                        down(k, j, p)
                        if first and j % 2 == 0:
                            project_attn(k // 2)

            expert_pair(0, first=True)
            with pe.Fori(1, E // 2 - 1) as i:
                expert_pair(i)
            expert_pair(E // 2 - 1, last=True)


def kernel(L0_attn_x, L0_attn_Wq, L0_attn_Wk, L0_attn_Wv, L0_attn_Wo, L0_ffn_router_weight, L0_ffn_router_bias,
           L0_ffn_w_gate, L0_ffn_w_up, L0_ffn_w_down):
    import numpy as np
    import concourse.bacc as bacc
    from concourse.bass_utils import run_bass_kernel_spmd

    arrays = {
        "x_in": L0_attn_x, "wq_in": L0_attn_Wq, "wk_in": L0_attn_Wk, "wv_in": L0_attn_Wv, "wo_in": np.transpose(np.reshape(L0_attn_Wo, (16, 16, 256)), (1, 0, 2)),
        "wr_in": np.transpose(L0_ffn_router_weight), "bias_in": L0_ffn_router_bias,
        "wg_in": np.transpose(L0_ffn_w_gate, (0, 2, 1)), "wu_in": np.transpose(L0_ffn_w_up, (0, 2, 1)),
        "wd_in": np.transpose(L0_ffn_w_down, (0, 2, 1)),
    }
    arrays = {name: np.ascontiguousarray(a) for name, a in arrays.items()}
    nc = bacc.Bacc("TRN2", target_bir_lowering=False, num_devices=1)
    ins = [nc.dram_tensor(name, a.shape, mybir.dt.from_np(a.dtype), kind="ExternalInput").ap() for name, a in arrays.items()]
    out = nc.dram_tensor("out", arrays["x_in"].shape, F32, kind="ExternalOutput").ap()
    build_layer(nc, *ins, out)
    result = run_bass_kernel_spmd(nc, [arrays], core_ids=[0])
    return result.results[0]["out"]
```

```python
from contextlib import ExitStack

import concourse.bass as bass
from concourse import mybir

F32 = mybir.dt.float32
F32R = mybir.dt.float32r
BF16 = mybir.dt.bfloat16
ALU = mybir.AluOpType
ACT = mybir.ActivationFunctionType
AX_X = mybir.AxisListType.X

P = 128
BANK = 512
LN_EPS = 1e-5
ROUTED_SCALE = 2.5
NEG_INF = -1.0e9
Q_PARTS = (0, 0, 1, 1, 0, 2)
K_PARTS = (0, 1, 0, 1, 2, 0)


def build_layer(nc, x, wq, wk, wv, wo, wr, bias, wg, wu, wd, out):
    NB, SEQ, D = x.shape
    T = NB * SEQ
    NT = T // P
    KC = D // P
    KV = wk.shape[1]
    HD = 16
    NH = D // HD
    NG = KV // HD
    REP = NH // NG
    E, _, I = wg.shape
    EG, PG = 4, E // 4
    NBLK = T // BANK
    TB = BANK // P
    SCALE = float(HD) ** -0.5
    NPART = len(Q_PARTS)
    KROWS = NPART * HD
    NGRP = NB * NG
    KT = SEQ // P
    QB = SEQ // BANK
    STEPS = QB * KT
    UNITS = STEPS * REP
    PAIRS = REP * KT
    AHEAD = 5
    SLOTS = (1, 2, 5, 8)
    PASS = (1, 104)
    TURN_AT = 111
    NEXT_PASS = (111, 20)
    EARLY = {4: 3, 5: 3, 6: 3}
    N_EARLY = sum(EARLY.values())
    EARLY_BANKS = (6, 0, 6)
    RING = 3
    WA = D + 2 * KV + E
    VR = KV + E
    WE = KC * I * 2 + D

    x_t = x.rearrange("b s d -> (b s) d").rearrange("(t p) d -> p t d", p=P)
    out_t = out.rearrange("b s d -> (b s) d").rearrange("(t p) d -> p t d", p=P)
    q_parts = nc.dram_tensor("q_parts", [3, NB * D, SEQ], BF16, kind="Internal").ap()
    k_parts = nc.dram_tensor("k_parts", [3, NB * KV, SEQ], BF16, kind="Internal").ap()
    attn_num = nc.dram_tensor("attn_num", [NB * D, SEQ], F32, kind="Internal").ap()
    attn_sum = nc.dram_tensor("attn_sum", [NB * NH, SEQ], F32, kind="Internal").ap()
    attn_inv = nc.dram_tensor("attn_inv", [NB * P, SEQ], F32, kind="Internal").ap()

    with ExitStack() as ctx:
        def sb(name, shape, dt, scope=ctx):
            return scope.enter_context(nc.sbuf_tensor(name, shape, dt))

        def sem(name):
            return ctx.enter_context(nc.semaphore(name))

        psum = ctx.enter_context(nc.psum_tensor("psum", [P, 8 * BANK], F32))
        banks = [psum[:, BANK * i:BANK * (i + 1)] for i in range(8)]

        X = sb("X", [P, NT, D], F32)
        xT_hi = sb("xT_hi", [P, KC, T], F32R)
        xT_lo = sb("xT_lo", [P, KC, T], F32R)
        V_all = sb("V_all", [P, NGRP, KT, HD], F32)
        logits = sb("logits", [P, NT, E], F32)
        scores = sb("scores", [P, NT, E], F32)
        combine = sb("combine", [P, NT, E], F32)
        ident = sb("ident", [P, P], F32)
        ident_bf = sb("ident_bf", [P, P], BF16)
        bias_sb = sb("bias_sb", [P, E], F32)
        earlier = sb("earlier", [P, EG, EG], F32)
        wo_hi = sb("wo_hi", [P, KC, D], F32R)
        wo_lo = sb("wo_lo", [P, KC, D], F32R)
        w_raw = [sb(f"w_raw{p}", [P, WE], F32) for p in range(2)]
        cnt = sb("cnt", [P, 3, NT], F32)

        sa = ExitStack()
        wa = sb("wa", [P, KC, WA], F32, sa)
        wa_hi = sb("wa_hi", [P, KC, WA], F32R, sa)
        wa_lo = sb("wa_lo", [P, KC, WA], F32R, sa)
        wo_sb = sb("wo_sb", [P, KC, D], F32, sa)
        xn = sb("xn", [P, TB, D], F32, sa)
        stats = sb("stats", [P, NT, 6], F32, sa)
        mv = sb("mv", [P, NT, 2], F32, sa)
        var_eps = sb("var_eps", [P, NT], F32, sa)
        std = sb("std", [P, NT], F32, sa)
        rstd0 = sb("rstd0", [P, NT], F32, sa)
        newton = sb("newton", [P, NT], F32, sa)
        rstd = sb("rstd", [P, NT], F32, sa)
        shift = sb("shift", [P, NT], F32, sa)
        part = [sb(f"part_{j}", [P, 3, BANK], BF16, sa) for j in range(3)]
        rest = [sb(f"rest_{j}", [P, BANK], F32, sa) for j in range(3)]
        sa.close()
        sc = ExitStack()
        num_sb = sb("num_sb", [P, 2, KC, BANK], F32, sc)
        inv_sb = sb("inv_sb", [P, 2, BANK], F32, sc)
        sums = sb("sums", [P, NB, SEQ * NH // P], F32, sc)
        inv = sb("inv", [P, NB, SEQ * NH // P], F32, sc)
        attn = sb("attn", [P, KC, BANK], F32, sc)
        attn_hi = sb("attn_hi", [P, KC, BANK], F32R, sc)
        attn_lo = sb("attn_lo", [P, KC, BANK], F32R, sc)
        sc.close()
        sa2 = ExitStack()
        of_a = KC * (3 * WA + D) + TB * D + NT * 14 + 3 * (3 * BANK // 2 + BANK)
        of_c = 2 * (KC + 1) * BANK + 2 * NB * SEQ * NH // P + 3 * KC * BANK
        sb("hold", [P, max(of_a, of_c) + 16], F32, sa2)
        bb = ExitStack()
        QS = [sb("QS0", [P, REP, SEQ], BF16, bb)]
        KS = [sb(f"KS{p}", [P, SEQ], BF16, bb) for p in range(RING)]
        V = [sb(f"V{p}", [P, KT, 2 * HD], F32, bb) for p in range(RING)]
        probs = [sb(f"probs{p}", [P, REP, BANK], F32, bb) for p in range(2)]
        qmax = sb("qmax", [P, PAIRS], F32, bb)
        mrest = sb("mrest", [P, PAIRS], F32, bb)
        mparts = sb("mparts", [P, 3, PAIRS], BF16, bb)
        mrows = sb("mrows", [3 * PAIRS, P], BF16, bb)
        O_sb = sb("O_sb", [P, QB, BANK], F32, bb)
        spare = probs[1][:, :, :].rearrange("p r t -> p (r t)").bitcast(BF16)
        parts = [[part[j][:, :, :] for j in range(3)],
                 [a.rearrange("p (i t) -> p i t", i=3) for a in
                  (spare[:, 0:3 * BANK], spare[:, 3 * BANK:6 * BANK],
                   O_sb[:, :, :].rearrange("p q t -> p (q t)").bitcast(BF16)[:, 0:3 * BANK])]]
        b2 = ExitStack()
        QS += [sb(f"QS{p}", [P, REP, SEQ], BF16, b2) for p in range(1, RING)]
        b2.close()
        rt = ExitStack()
        choice = sb("choice", [P, NT, EG, PG], F32, rt)
        work1 = sb("work1", [P, NT, E], F32, rt)
        work2 = sb("work2", [P, NT, E], F32, rt)
        work3 = sb("work3", [P, NT, E], F32, rt)
        top8 = sb("top8", [P, NT, 8], F32, rt)
        gsc = sb("gsc", [P, NT, EG], F32, rt)
        small = sb("small", [P, 4, NT, EG], F32, rt)
        w_lo0 = sb("w_lo0", [P, WE], F32R, rt)
        rt.close()
        bb.close()
        se = ExitStack()
        act_g = [sb(f"act_g{p}", [P, BANK], F32, se) for p in range(2)]
        h = [sb(f"h{p}", [P, BANK], F32, se) for p in range(2)]
        h_hi = [sb("h_hi0", [P, BANK], F32R, se)]
        w_hi = [sb("w_hi0", [P, WE], F32R, se)]
        h_hi += [sb("h_hi1", [P, BANK], F32R, se)]
        h_lo = [sb(f"h_lo{p}", [P, BANK], F32R, se) for p in range(2)]
        w_hi += [sb("w_hi1", [P, WE], F32R, se)]
        w_lo = [w_lo0, sb("w_lo1", [P, WE], F32R, se)]
        se.close()
        sa2.close()

        x_loaded = [sem(f"x_loaded{c}") for c in range(NBLK)]
        w_loaded, wo_loaded = sem("w_loaded"), sem("wo_loaded")
        warm = sem("warm")
        consts = sem("consts")
        wa_hi_done, wa_lo_done = sem("wa_hi_done"), sem("wa_lo_done")
        ln_step = sem("ln_step")
        ve_done, std_done, rstd_done, xn_done = sem("ve_done"), sem("std_done"), sem("rstd_done"), sem("xn_done")
        tp_done, hi_done, lo_done = sem("tp_done"), sem("hi_done"), sem("lo_done")
        qk_done, vr_done, vr_read = sem("qk_done"), sem("vr_done"), sem("vr_read")
        p1_done, rest_done, p2_done, p3_done = sem("p1_done"), sem("rest_done"), sem("p2_done"), sem("p3_done")
        parts_stored = [sem("parts_stored0"), sem("parts_stored1")]
        stacks_loaded = [sem(f"stacks_loaded{p}") for p in range(RING)]
        v_loaded = [sem(f"v_loaded{p}") for p in range(RING)]
        negmax_loaded = sem("negmax_loaded")
        mx_done, mx_read = sem("mx_done"), sem("mx_read")
        chain = sem("chain")
        mparts_done, mT_done, mrows_done = sem("mparts_done"), sem("mT_done"), sem("mrows_done")
        st_done, exp_done, pv_done = sem("st_done"), sem("exp_done"), sem("pv_done")
        o_done, o_stored = sem("o_done"), sem("o_stored")
        scores_done, route = sem("scores_done"), sem("route")
        attn_loaded = [sem("attn_loaded0"), sem("attn_loaded1")]
        sums_loaded, inv_done, inv_stored = sem("sums_loaded"), sem("inv_done"), sem("inv_stored")
        attn_done, ahi_done, alo_done = sem("attn_done"), sem("ahi_done"), sem("alo_done")
        y_done, acc_done = sem("y_done"), sem("acc_done")
        we_loaded = [sem("we_loaded0"), sem("we_loaded1")]
        whi_done, wlo_done = sem("whi_done"), sem("wlo_done")
        g_done, u_done, silu_done = sem("g_done"), sem("u_done"), sem("silu_done")
        h_done, hhi_done, hlo_done = sem("h_done"), sem("hhi_done"), sem("hlo_done")
        stored = sem("stored")

        EXP0 = UNITS
        PV0 = 2
        O0 = 1

        def bank_of(u, p, last):
            return u % 7 if last else (u + p) % 3

        def pair_bank(v):
            return 5 - 2 * (v % 2)

        def places(where, count):
            first, span = where
            return [first + span * i / count for i in range(count)]

        def slot(s, i):
            return 2 * REP * s + (SLOTS[i - 1] if i else 0), 2 * REP * s + SLOTS[i]

        def turn(k):
            return k + k // 2 if isinstance(k, int) and k < 2 * NBLK else k + NBLK

        def three(pe, to, lhs, rhs):
            terms = [(l, r) for (lh, ll), (rh, rl) in zip(lhs, rhs) for l, r in ((lh, rh), (lh, rl), (ll, rh))]
            for i, (l, r) in enumerate(terms):
                last = pe.matmul(to, l, r, start=(i == 0), stop=(i == len(terms) - 1))
            return last

        block = ctx.enter_context(nc.Block())

        @block.sync
        def _(sp):
            for c in range(NBLK):
                if c == 2:
                    sp.wait_ge(w_loaded, 64)
                sp.dma_start(X[:, TB * c:TB * (c + 1), :], x_t[:, TB * c:TB * (c + 1), :]).then_inc(x_loaded[c], 16)
            def store_parts(n):
                for j in range(3):
                    M = P if j < 2 else KV
                    dst, row = (q_parts, D * (n // 2) + P * j) if j < 2 else (k_parts, KV * (n // 2))
                    for done in (p1_done, p2_done, p3_done):
                        sp.wait_ge(done, 3 * n + j + 1)
                    sp.dma_start(dst[:, row:row + M, BANK * (n % 2):BANK * (n % 2 + 1)].rearrange("i p t -> p i t"),
                                 parts[n % 2][j][0:M, :, :]).then_inc(parts_stored[n % 2], 16)

            def load_stacks(m, p):
                for s, (i, j) in enumerate(zip(Q_PARTS, K_PARTS)):
                    sp.dma_start(QS[p][HD * s:HD * (s + 1), :, :],
                                 q_parts[i, bass.ds(m * (REP * HD), REP * HD), :].rearrange("(h d) t -> d h t", d=HD)
                                 ).then_inc(stacks_loaded[p], 16)
                    sp.dma_start(KS[p][HD * s:HD * (s + 1), :],
                                 k_parts[j, bass.ds(m * HD, HD), :]).then_inc(stacks_loaded[p], 16)

            def load_v(m, p):
                sp.dma_start(V[p][:, :, 0:HD], V_all[:, bass.ds(m, 1), :, :].rearrange("p m t d -> p (m t) d")
                             ).then_inc(v_loaded[p], 16)

            def negmax(m, p):
                sp.wait_ge(mrows_done, m + 1)
                sp.dma_start(QS[p][KROWS:KROWS + 3, :, :].rearrange("a h (t q) -> a (h t) q", q=P),
                             mrows[:, :]).then_inc(negmax_loaded, 16)

            def next_loads(n, p):
                sp.wait_ge(st_done, UNITS * n + UNITS)
                for q in range(2):
                    sp.wait_ge(parts_stored[q], 16 * 3 * NBLK // 2)
                load_stacks(n + RING, p)
                sp.wait_ge(pv_done, STEPS * n + STEPS + PV0)
                sp.wait_ge(vr_read, 2 * NBLK)
                load_v(n + RING, p)

            for n in range(NBLK):
                store_parts(n)
                if n == 1:
                    for q in range(2):
                        sp.wait_ge(parts_stored[q], 16 * 3)
                    load_stacks(0, 0)
            sp.wait_ge(vr_read, 2 * 2)
            load_v(0, 0)
            for p in range(1, RING):
                load_stacks(p, p)
                load_v(p, p)
            negmax(0, 0)
            with sp.Fori(0, NGRP // RING - 1) as i:
                for p in range(RING):
                    negmax(RING * i + p + 1, (p + 1) % RING)
                    next_loads(RING * i + p, p)
            for n in range(NGRP - 1 - RING, NGRP - 1):
                negmax(n + 1, (n + 1) % RING)
                if n + RING < NGRP:
                    next_loads(n, n % RING)

            num_v = attn_num.rearrange("(b k p) t -> b p k t", p=P, k=KC)
            inv_v = attn_inv.rearrange("(b p) t -> b p t", p=P)
            sum_c = attn_sum.rearrange("(b h) (s c) -> (h s) b c", b=NB, c=P)
            inv_c = attn_inv.rearrange("(b d h) (s c) -> b (h s) d c", b=NB, h=NH, c=P)

            def load_sums(b0, b1):
                sp.wait_ge(o_stored, 16 * 2 * REP * NG * b1)
                sp.dma_start(sums[:, b0:b1, :], sum_c[:, b0:b1, :]).then_inc(sums_loaded, 16)

            def store_inverses(b0, b1, count):
                sp.wait_ge(inv_done, count)
                for b in range(b0, b1):
                    sp.dma_start(inv_c[b], inv[:, b, :].unsqueeze(1).broadcast_to([P, HD // KC, P])).then_inc(inv_stored, 16)
                sp.wait_ge(inv_stored, 16 * b1)

            def load_attn(n):
                b, cols = n // 2, slice(BANK * (n % 2), BANK * (n % 2 + 1))
                sp.dma_start(num_sb[:, n % 2, :, :], num_v[b, :, :, cols]).then_inc(attn_loaded[n % 2], 16)
                sp.dma_start(inv_sb[:, n % 2, :], inv_v[b, :, cols]).then_inc(attn_loaded[n % 2], 16)

            def load_expert(e, p):
                w = w_raw[p]
                sp.dma_start(w[:, 0:KC * I].rearrange("p (k i) -> p k i", k=KC),
                             wg[bass.ds(e, 1), :, :].rearrange("e (k p) i -> p (e k) i", p=P)).then_inc(we_loaded[p], 16)
                sp.dma_start(w[:, KC * I:2 * KC * I].rearrange("p (k i) -> p k i", k=KC),
                             wu[bass.ds(e, 1), :, :].rearrange("e (k p) i -> p (e k) i", p=P)).then_inc(we_loaded[p], 16)
                sp.dma_start(w[:, 2 * KC * I:WE],
                             wd[bass.ds(e, 1), :, :].rearrange("e i d -> i (e d)")).then_inc(we_loaded[p], 16)

            load_expert(0, 0)
            load_expert(1, 1)
            load_sums(0, NB - 1)
            store_inverses(0, NB - 1, 1)
            load_attn(0)
            load_attn(1)
            load_sums(NB - 1, NB)

            def refill(e, p):
                sp.wait_ge(whi_done, e - 1)
                sp.wait_ge(wlo_done, e - 1)
                load_expert(e, p)

            for n in range(2, NBLK):
                sp.wait_ge(attn_done, n - 1)
                load_attn(n)
                if n <= 3:
                    refill(n, n - 2)
                if n == 3:
                    store_inverses(NB - 1, NB, 2)
            with sp.Fori(2, E // 2) as i:
                for p in range(2):
                    refill(2 * i + p, p)
            for n in range(NBLK):
                sp.wait_ge(acc_done, TB * (turn((E - 1) * NBLK + n) + 1))
                sp.dma_start(out_t[:, TB * n:TB * (n + 1), :], X[:, TB * n:TB * (n + 1), :]).then_inc(stored, 16)
            sp.wait_ge(stored, 16 * NBLK)

        @block.gpsimd
        def _(pool):
            pool.memset(ident[:, :], 0.0).then_inc(consts, 1)
            pool.memset(earlier[:, :, :], 1.0).then_inc(consts, 1)
            for p in range(RING):
                pool.memset(V[p][:, :, HD:2 * HD], 1.0).then_inc(v_loaded[p], 16)
            pool.wait_ge(consts, 2)
            pool.wait_ge(warm, 1)
            pool.affine_select(out=ident[:, :], in_=ident[:, :], compare_op=ALU.not_equal, fill=1.0, base=0,
                               pattern=[[-1, P]], channel_multiplier=1).then_inc(consts, 1)
            pool.affine_select(out=earlier[:, :, :], in_=earlier[:, :, :], compare_op=ALU.is_gt, fill=0.0, base=0,
                               pattern=[[1, EG], [-1, EG]], channel_multiplier=0).then_inc(consts, 1)
            for n in range(NBLK):
                for j in range(3):
                    M = P if j < 2 else KV
                    u = 3 * n + j
                    if n >= 2:
                        pool.wait_ge(parts_stored[n % 2], 16 * 3 * (n // 2))
                    pool.wait_ge(p2_done, u + 1)
                    pool.wait_ge(rest_done, u + 1)
                    pool.tensor_tensor(parts[n % 2][j][0:M, 2, :], rest[j][0:M, :], parts[n % 2][j][0:M, 1, :],
                                       ALU.subtract).then_inc(p3_done, 1)
            num_h = attn_num.rearrange("(b d h) t -> b h d t", b=NB, h=NH)
            def store_results(b, g):
                n = b * NG + g
                pool.wait_ge(o_done, 2 * n + 2 + O0)
                for r in range(REP):
                    at = 2 * HD * r
                    pool.dma_start(num_h[bass.ds(b, 1), REP * g + r, :, :].rearrange("a d t -> (a d) t"),
                                   O_sb[at:at + HD, :, :]).then_inc(o_stored, 16)
                    pool.dma_start(attn_sum[bass.ds(n * REP + r, 1), :],
                                   O_sb[at + HD:at + HD + 1, :, :]).then_inc(o_stored, 16)

            def normalise_attn(n):
                pool.wait_ge(attn_loaded[n % 2], 32 * (n // 2 + 1))
                if n >= 1:
                    pool.wait_ge(ahi_done, n)
                    pool.wait_ge(alo_done, n)
                pool.tensor_tensor(attn[:, :, :], num_sb[:, n % 2, :, :],
                                   inv_sb[:, n % 2, :].unsqueeze(1).broadcast_to([P, KC, BANK]), ALU.mult).then_inc(attn_done, 1)

            with pool.Fori(0, NB - 1) as b:
                for g in range(NG):
                    store_results(b, g)
            for g in range(NG - 1):
                store_results(NB - 1, g)
            normalise_attn(0)
            store_results(NB - 1, NG - 1)
            for n in range(1, NBLK):
                normalise_attn(n)

        @block.scalar
        def _(act):
            act.dma_start(wa[:, :, 0:D], wq.rearrange("(k p) n -> p k n", p=P)).then_inc(w_loaded, 16)
            act.dma_start(wa[:, :, D:D + KV], wk.rearrange("(k p) n -> p k n", p=P)).then_inc(w_loaded, 16)
            act.dma_start(wa[:, :, D + KV:D + 2 * KV], wv.rearrange("(k p) n -> p k n", p=P)).then_inc(w_loaded, 16)
            act.dma_start(wa[:, :, D + 2 * KV:WA], wr.rearrange("(k p) n -> p k n", p=P)).then_inc(w_loaded, 16)
            act.wait_ge(consts, 1)
            act.activation(cnt[:, 0, 0:1], ident[:, 0:1], ACT.Sqrt).then_inc(warm, 1)
            act.dma_start(wo_sb[:, :, :], wo.rearrange("d h n -> (d h) n").rearrange("(k p) n -> p k n", p=P)).then_inc(wo_loaded, 16)
            act.dma_start(bias_sb[:, :], bias.rearrange("(a n) -> a n", a=1).broadcast_to([P, E])).then_inc(wo_loaded, 16)

            def root(c):
                act.wait_ge(ve_done, c + 1)
                act.activation(std[:, TB * c:TB * (c + 1)], var_eps[:, TB * c:TB * (c + 1)], ACT.Sqrt).then_inc(std_done, 1)

            def normalise(c):
                act.wait_ge(rstd_done, c + 1)
                for i in range(TB):
                    t = TB * c + i
                    if c >= 1:
                        act.wait_ge(tp_done, 2 * (c - 1) + i // 2 + 1)
                    act.activation(xn[:, i, :], X[:, t, :], ACT.Identity, bias=shift[:, t:t + 1],
                                   scale=rstd[:, t:t + 1]).then_inc(xn_done, 1)

            def hi_of_x(c):
                for q in range(2 * c, 2 * c + 2):
                    act.wait_ge(tp_done, q + 1)
                    act.activation(xT_hi[:, :, 2 * P * q:2 * P * (q + 1)],
                                   banks[q % 2].rearrange("p (k t) -> p k t", k=KC), ACT.Copy).then_inc(hi_done, 1)

            root(0)
            normalise(0)
            root(1)
            act.wait_ge(w_loaded, 64)
            act.activation(wa_hi[:, :, :], wa[:, :, :], ACT.Copy).then_inc(wa_hi_done, 1)
            hi_of_x(0)
            normalise(1)
            root(2)
            root(3)
            act.wait_ge(wo_loaded, 32)
            act.activation(wo_hi[:, :, :], wo_sb[:, :, :], ACT.Copy).then_inc(wa_hi_done, 1)
            for c in range(NBLK):
                if c >= 2:
                    act.wait_ge(parts_stored[c % 2], 16 * 3 * (c // 2))
                for j in range(3):
                    M = P if j < 2 else KV
                    act.wait_ge(qk_done, 3 * c + j + 1)
                    act.activation(parts[c % 2][j][0:M, 0, :], banks[2 + j][0:M, :], ACT.Copy).then_inc(p1_done, 1)
                if c + 1 < NBLK:
                    hi_of_x(c + 1)
                if c + 2 < NBLK:
                    normalise(c + 2)
                for j in range(3):
                    M = P if j < 2 else KV
                    act.wait_ge(rest_done, 3 * c + j + 1)
                    act.activation(parts[c % 2][j][0:M, 1, :], rest[j][0:M, :], ACT.Copy).then_inc(p2_done, 1)
                if c + 4 < NBLK:
                    root(c + 4)
                act.wait_ge(vr_done, c + 1)
                vr = banks[5][:, 0:TB * VR].rearrange("p (t n) -> p t n", t=TB)
                act.activation(V_all[:, NG * (c // 2):NG * (c // 2 + 1), TB * (c % 2):TB * (c % 2 + 1), :].rearrange("p g t d -> p t g d"),
                               vr[:, :, 0:KV].rearrange("p t (g d) -> p t g d", d=HD), ACT.Copy).then_inc(vr_read, 1)
                act.activation(logits[:, TB * c:TB * (c + 1), :], vr[:, :, KV:VR], ACT.Copy).then_inc(vr_read, 1)
            act.wait_ge(vr_read, 2 * NBLK)
            act.activation(scores[:, :, :], logits[:, :, :], ACT.Sigmoid).then_inc(scores_done, 1)

            def exps(n, p):
                last = isinstance(n, int) and n == NGRP - 1
                for s in range(STEPS):
                    for r in range(REP):
                        u = REP * s + r
                        if r == 0:
                            act.wait_ge(pv_done, STEPS * n + s - 1 + PV0)
                        act.wait_ge(st_done, UNITS * n + u + 1)
                        act.activation(probs[s % 2][:, r, :], banks[bank_of(u, p, last)][:, :], ACT.Exp, scale=SCALE).then_inc(exp_done, 1)

            act.wait_ge(parts_stored[1], 16 * 3 * NBLK // 2)
            with act.Fori(0, NGRP // RING) as i:
                for p in range(RING):
                    exps(RING * i + p, p)
            for n in range(NGRP // RING * RING, NGRP):
                exps(n, n % RING)

            def hi_of_attn(n):
                act.wait_ge(attn_done, n + 1)
                if n >= 1:
                    act.wait_ge(y_done, 2 * turn(2 * n - 1) + 4)
                act.activation(attn_hi[:, :, :], attn[:, :, :], ACT.Copy).then_inc(ahi_done, 1)

            def w_split(p, loads):
                act.wait_ge(we_loaded[p], loads)
                act.activation(w_hi[p][:, :], w_raw[p][:, :], ACT.Copy).then_inc(whi_done, 1)

            def silu(k, par, first=False):
                act.wait_ge(g_done, k + 1)
                if not first:
                    act.wait_ge(h_done, k - 1)
                act.activation(act_g[par][:, :], banks[par][:, :], ACT.Silu).then_inc(silu_done, 1)

            def hi_of_h(k, par, first=False):
                act.wait_ge(h_done, k + 1)
                if not first:
                    act.wait_ge(y_done, 2 * turn(k - 2) + 2)
                act.activation(h_hi[par][:, :], h[par][:, :], ACT.Copy).then_inc(hhi_done, 1)

            act.wait_ge(pv_done, STEPS * NGRP + PV0)
            silu(0, 0, True)
            hi_of_h(0, 0, True)

            def expert_pair(i, last=False, first=False):
                for p in range(2):
                    for j in range(NBLK):
                        k = 2 * NBLK * i + NBLK * p + j
                        final = last and p == 1
                        if j == 1 and not final:
                            act.wait_ge(y_done, 2 * turn(max(k - 2, 0) if first else k - 2) + 2)
                            w_split(1 - p, 48 * i + 48 * p + 48)
                        if not (final and j == NBLK - 1):
                            silu(k + 1, (j + 1) % 2, first and k == 0)
                            hi_of_h(k + 1, (j + 1) % 2, first and k == 0)
                        if first and j % 2 == 0:
                            hi_of_attn(k // 2)

            expert_pair(0, first=True)
            with act.Fori(1, E // 2 - 1) as i:
                expert_pair(i)
            expert_pair(E // 2 - 1, last=True)

        @block.vector
        def _(dve):
            dve.memset(KS[0][KROWS:P, :], 1.0).then_inc(exp_done, EXP0)
            dve.memset(KS[1][KROWS:P, :], 1.0).then_inc(pv_done, PV0)
            dve.memset(KS[2][KROWS:P, :], 1.0).then_inc(o_done, O0)
            step = [0]

            def link(ins, s=ln_step):
                ins.then_inc(s, 1)
                step[0] += 1
                dve.wait_ge(s, step[0])

            def ln_stats(c):
                tiles = range(TB * c, TB * (c + 1))
                sl = slice(TB * c, TB * (c + 1))
                dve.wait_ge(x_loaded[c], 16)
                for t in tiles:
                    last = dve.bn_stats(stats[:, t, :], X[:, t, :])
                link(last)
                for t in tiles:
                    last = dve.bn_aggr(mv[:, t, :], stats[:, t, :])
                link(last)
                dve.tensor_scalar(var_eps[:, sl], mv[:, sl, 1], LN_EPS, None, ALU.add).then_inc(ve_done, 1)

            def ln_scale(c):
                sl = slice(TB * c, TB * (c + 1))
                dve.wait_ge(std_done, c + 1)
                dve.wait_ge(ve_done, c + 1)
                link(dve.reciprocal(rstd0[:, sl], std[:, sl]))
                link(dve.tensor_tensor(newton[:, sl], rstd0[:, sl], rstd0[:, sl], ALU.mult))
                link(dve.tensor_tensor(newton[:, sl], newton[:, sl], var_eps[:, sl], ALU.mult))
                link(dve.tensor_scalar(newton[:, sl], newton[:, sl], -0.5, 1.5, ALU.mult, ALU.add))
                link(dve.tensor_tensor(rstd[:, sl], rstd0[:, sl], newton[:, sl], ALU.mult))
                dve.scalar_tensor_tensor(out=shift[:, sl], in0=mv[:, sl, 0], scalar=-1.0, in1=rstd[:, sl],
                                         op0=ALU.mult, op1=ALU.mult).then_inc(rstd_done, 1)

            ln_stats(0)
            dve.wait_ge(consts, 4)
            dve.tensor_copy(ident_bf[:, :], ident[:, :]).then_inc(consts, 1)
            ln_scale(0)
            ln_stats(1)
            ln_scale(1)

            def lo_of_x(c):
                for q in range(2 * c, 2 * c + 2):
                    dve.wait_ge(hi_done, q + 1)
                    cols = slice(2 * P * q, 2 * P * (q + 1))
                    dve.tensor_tensor(xT_lo[:, :, cols], banks[q % 2].rearrange("p (k t) -> p k t", k=KC),
                                      xT_hi[:, :, cols].bitcast(F32), ALU.subtract).then_inc(lo_done, 1)

            dve.wait_ge(wa_hi_done, 1)
            dve.tensor_tensor(wa_lo[:, :, :], wa[:, :, :], wa_hi[:, :, :].bitcast(F32), ALU.subtract).then_inc(wa_lo_done, 1)
            lo_of_x(0)
            ln_stats(2)
            ln_stats(3)
            ln_scale(2)
            dve.wait_ge(wa_hi_done, 2)
            dve.tensor_tensor(wo_lo[:, :, :], wo_sb[:, :, :], wo_hi[:, :, :].bitcast(F32), ALU.subtract).then_inc(wa_lo_done, 1)
            def maximum(m, v, bank):
                dve.wait_ge(mx_done, PAIRS * m + v + 1)
                at = BANK * bank
                dve.tensor_reduce(qmax[:, v:v + 1], psum[:, at:at + 2 * BANK], AX_X, ALU.max).then_inc(mx_read, 1)

            early = iter(range(N_EARLY))
            for c in range(NBLK):
                for j in range(3):
                    M = P if j < 2 else KV
                    u = 3 * c + j
                    dve.wait_ge(p1_done, u + 1)
                    if c >= 1:
                        dve.wait_ge(p3_done, u - 2)
                    dve.tensor_tensor(rest[j][0:M, :], banks[2 + j][0:M, :], parts[c % 2][j][0:M, 0, :],
                                      ALU.subtract).then_inc(rest_done, 1)
                if c + 1 < NBLK:
                    lo_of_x(c + 1)
                for i in range(EARLY.get(c, 0)):
                    maximum(0, next(early), EARLY_BANKS[i])
                if c + 3 < NBLK:
                    ln_scale(c + 3)
                if c + 4 < NBLK:
                    ln_stats(c + 4)

            soon = AHEAD + sum(at <= SLOTS[2] for at in places(PASS, PAIRS - AHEAD)) - 1
            middle = AHEAD + sum(at <= 2 * REP * KT + SLOTS[2] for at in places(PASS, PAIRS - AHEAD)) - 1

            def maxima(m, start=AHEAD):
                for v in range(start, PAIRS):
                    maximum(m, v, pair_bank(v))
                    if v == soon and not (isinstance(m, int) and m <= 1):
                        output(m - 2, 1)
                    if v == middle and not (isinstance(m, int) and m == 0):
                        output(m - 1, 0)
                dve.wait_ge(mx_read, PAIRS * m + PAIRS)
                dve.tensor_scalar(mparts[:, 0, :], qmax[:, :], -1.0, None, ALU.mult).then_inc(chain, 1)
                dve.wait_ge(chain, 3 * m + 1)
                dve.scalar_tensor_tensor(out=mrest[:, :], in0=qmax[:, :], scalar=-1.0, in1=mparts[:, 0, :],
                                         op0=ALU.mult, op1=ALU.subtract).then_inc(chain, 1)
                dve.wait_ge(chain, 3 * m + 2)
                dve.tensor_copy(mparts[:, 1, :], mrest[:, :]).then_inc(chain, 1)
                dve.wait_ge(chain, 3 * m + 3)
                dve.tensor_tensor(mparts[:, 2, :], mrest[:, :], mparts[:, 1, :], ALU.subtract).then_inc(mparts_done, 1)
                dve.wait_ge(mT_done, m + 1)
                dve.wait_ge(negmax_loaded, 16 * m)
                dve.tensor_copy(mrows[:, :], banks[3][0:3 * PAIRS, 0:P // 2].bitcast(BF16)).then_inc(mrows_done, 1)

            def output(n, qb):
                dve.wait_ge(pv_done, STEPS * n + KT * (qb + 1) + PV0)
                if not isinstance(n, int) or n > 0:
                    dve.wait_ge(o_stored, 16 * 2 * REP * n)
                dve.tensor_copy(O_sb[:, qb, :], banks[7]).then_inc(o_done, 1)

            def first_maxima(m):
                for v in range(AHEAD):
                    maximum(m, v, pair_bank(v))

            maxima(0, start=N_EARLY)
            first_maxima(1)
            maxima(1)
            first_maxima(2)
            with dve.Fori(2, NGRP - 1) as m:
                maxima(m)
                first_maxima(m + 1)
            maxima(NGRP - 1)
            output(NGRP - 2, 1)

            step[0] = 0
            r_ = lambda ins: link(ins, route)
            dve.wait_ge(scores_done, 1)
            dve.wait_ge(st_done, UNITS * (NGRP - 1))
            sc4 = scores[:, :, :].rearrange("p t (g e) -> p t g e", g=EG)
            b4 = bias_sb[:, :].rearrange("p (a g e) -> p a g e", a=1, g=EG).broadcast_to([P, NT, EG, PG])
            r_(dve.tensor_tensor(choice[:, :, :, :], sc4, b4, ALU.add))
            c_lo, c_hi = choice[:, :, :, 0:PG:2], choice[:, :, :, 1:PG:2]
            pair_max = work1[:, :, 0:2 * EG].rearrange("p t (g e) -> p t g e", g=EG)
            pair_min = work2[:, :, 0:2 * EG].rearrange("p t (g e) -> p t g e", g=EG)
            r_(dve.tensor_tensor(pair_max, c_lo, c_hi, ALU.max))
            r_(dve.tensor_tensor(pair_min, c_lo, c_hi, ALU.min))
            first, second, third = small[:, 0, :, :], small[:, 1, :, :], small[:, 2, :, :]
            r_(dve.tensor_tensor(first, pair_max[:, :, :, 0], pair_max[:, :, :, 1], ALU.max))
            r_(dve.tensor_tensor(second, pair_max[:, :, :, 0], pair_max[:, :, :, 1], ALU.min))
            r_(dve.tensor_tensor(third, pair_min[:, :, :, 0], pair_min[:, :, :, 1], ALU.max))
            r_(dve.tensor_tensor(second, second, third, ALU.max))
            r_(dve.tensor_tensor(gsc[:, :, :], first, second, ALU.add))
            other = gsc[:, :, :].unsqueeze(2).broadcast_to([P, NT, EG, EG])
            own = gsc[:, :, :].unsqueeze(3).broadcast_to([P, NT, EG, EG])
            more = work1[:, :, :].rearrange("p t (g e) -> p t g e", g=EG)
            same = work2[:, :, :].rearrange("p t (g e) -> p t g e", g=EG)
            lower = earlier[:, :, :].unsqueeze(1).broadcast_to([P, NT, EG, EG])
            r_(dve.tensor_tensor(more, other, own, ALU.is_gt))
            r_(dve.tensor_tensor(same, other, own, ALU.is_equal))
            r_(dve.tensor_tensor(same, same, lower, ALU.mult))
            r_(dve.tensor_tensor(more, more, same, ALU.add))
            rank, keep, drop = small[:, 0, :, :], small[:, 1, :, :], small[:, 2, :, :]
            r_(dve.tensor_reduce(rank, more, AX_X, ALU.add))
            r_(dve.tensor_scalar(keep, rank, 2.0, None, ALU.is_lt))
            r_(dve.tensor_scalar(drop, keep, -NEG_INF, NEG_INF, ALU.mult, ALU.add))
            wide = lambda a: a.unsqueeze(3).broadcast_to([P, NT, EG, PG])
            r_(dve.tensor_tensor(choice[:, :, :, :], choice[:, :, :, :], wide(keep), ALU.mult))
            r_(dve.tensor_tensor(choice[:, :, :, :], choice[:, :, :, :], wide(drop), ALU.add))
            masked = choice[:, :, :, :].rearrange("p t g e -> p t (g e)")
            for t in range(NT):
                last = dve.max(top8[:, t, :], masked[:, t, :])
            r_(last)
            fourth = top8[:, :, 3:4].broadcast_to([P, NT, E])
            above, equal, run = work1[:, :, :], work2[:, :, :], work3[:, :, :]
            r_(dve.tensor_tensor(above, masked, fourth, ALU.is_gt))
            r_(dve.tensor_tensor(equal, masked, fourth, ALU.is_equal))
            r_(dve.tensor_reduce(cnt[:, 0, :], above, AX_X, ALU.add))
            r_(dve.tensor_scalar(cnt[:, 1, :], cnt[:, 0, :], -1.0, 4.0, ALU.mult, ALU.add))
            src, dst = equal, run
            for d in (1, 2, 4, 8):
                if d == 8:
                    output(NGRP - 1, 0)
                r_(dve.tensor_copy(dst[:, :, 0:d], src[:, :, 0:d]))
                r_(dve.tensor_tensor(dst[:, :, d:E], src[:, :, d:E], src[:, :, 0:E - d], ALU.add))
                if d == 1:
                    src, dst = run, combine[:, :, :]
                else:
                    src, dst = dst, src
            counted, free = src, dst
            r_(dve.tensor_tensor(free, counted, cnt[:, 1, :].unsqueeze(2).broadcast_to([P, NT, E]), ALU.is_le))
            r_(dve.tensor_tensor(free, free, equal, ALU.mult))
            r_(dve.tensor_tensor(above, above, free, ALU.add))
            r_(dve.tensor_tensor(above, above, scores[:, :, :], ALU.mult))
            r_(dve.tensor_reduce(cnt[:, 0, :], above, AX_X, ALU.add))
            r_(dve.tensor_scalar(cnt[:, 0, :], cnt[:, 0, :], 1e-20, None, ALU.add))
            r_(dve.reciprocal(cnt[:, 2, :], cnt[:, 0, :]))
            r_(dve.tensor_scalar(cnt[:, 2, :], cnt[:, 2, :], ROUTED_SCALE, None, ALU.mult))
            r_(dve.tensor_tensor(combine[:, :, :], above, cnt[:, 2, :].unsqueeze(2).broadcast_to([P, NT, E]), ALU.mult))

            def inverses(b0, b1, count):
                dve.wait_ge(sums_loaded, 16 * count)
                dve.reciprocal(inv[:, b0:b1, :], sums[:, b0:b1, :]).then_inc(inv_done, 1)

            inverses(0, NB - 1, 1)
            dve.wait_ge(we_loaded[0], 48)
            dve.tensor_copy(w_hi[0][:, :], w_raw[0][:, :]).then_inc(whi_done, 1)
            dve.wait_ge(whi_done, 1)
            dve.tensor_tensor(w_lo[0][:, :], w_raw[0][:, :], w_hi[0][:, :].bitcast(F32), ALU.subtract).then_inc(wlo_done, 1)
            output(NGRP - 1, 1)

            def lo_of_attn(n):
                dve.wait_ge(ahi_done, n + 1)
                if n >= 1:
                    dve.wait_ge(y_done, 2 * turn(2 * n - 1) + 4)
                dve.tensor_tensor(attn_lo[:, :, :], attn[:, :, :], attn_hi[:, :, :].bitcast(F32), ALU.subtract).then_inc(alo_done, 1)

            def y(turns, t):
                return banks[4 + 2 * (turns % 2) + t // 2][:, D * (t % 2):D * (t % 2 + 1)]

            added = {}

            def add_attn(n):
                r = turn(2 * n + 1) + 1
                for t in range(TB):
                    dve.wait_ge(y_done, 2 * r + t // 2 + 1)
                    if n in added:
                        dve.wait_ge(acc_done, TB * added[n] + t + 1)
                    xt = X[:, TB * n + t, :]
                    dve.tensor_tensor(xt, y(r, t), xt, ALU.add).then_inc(acc_done, 1)
                added[n] = r

            def w_split(p, count):
                dve.wait_ge(whi_done, count)
                dve.tensor_tensor(w_lo[p][:, :], w_raw[p][:, :], w_hi[p][:, :].bitcast(F32), ALU.subtract).then_inc(wlo_done, 1)

            def gated(k, par, first=False):
                dve.wait_ge(u_done, k + 1)
                dve.wait_ge(silu_done, k + 1)
                if not first:
                    dve.wait_ge(hhi_done, k - 1)
                    dve.wait_ge(hlo_done, k - 1)
                dve.tensor_tensor(h[par][:, :], banks[2 + par][:, :], act_g[par][:, :], ALU.mult).then_inc(h_done, 1)
                dve.wait_ge(hhi_done, k + 1)
                dve.tensor_tensor(h_lo[par][:, :], h[par][:, :], h_hi[par][:, :].bitcast(F32), ALU.subtract).then_inc(hlo_done, 1)

            def add_expert(k, j, e):
                r = turn(k)
                for t in range(TB):
                    dve.wait_ge(y_done, 2 * r + t // 2 + 1)
                    if not isinstance(k, int):
                        dve.wait_ge(acc_done, TB * r + t - TB)
                    elif j in added:
                        dve.wait_ge(acc_done, TB * added[j] + t + 1)
                    tile = TB * j + t
                    dve.scalar_tensor_tensor(out=X[:, tile, :], in0=y(r if isinstance(r, int) else j, t),
                                             scalar=combine[:, tile, bass.ds(e, 1)], in1=X[:, tile, :],
                                             op0=ALU.mult, op1=ALU.add).then_inc(acc_done, 1)
                if isinstance(r, int):
                    added[j] = r

            gated(0, 0, True)

            def expert_pair(i, last=False, first=False):
                for p in range(2):
                    for j in range(NBLK):
                        k = 2 * NBLK * i + NBLK * p + j
                        final = last and p == 1
                        if j == 1 and not final:
                            w_split(1 - p, 2 * i + p + 2)
                        if not (final and j == NBLK - 1):
                            gated(k + 1, (j + 1) % 2, first and k == 0)
                        if first and j % 2 == 0:
                            lo_of_attn(k // 2)
                        add_expert(k, j, 2 * i + p)
                        if first and j % 2 == 1:
                            add_attn(k // 2)
                        if first and k == 3:
                            inverses(NB - 1, NB, 2)

            expert_pair(0, first=True)
            added.clear()
            with dve.Fori(1, E // 2 - 1) as i:
                expert_pair(i)
            for j in range(NBLK):
                added[j] = turn((E - 3) * NBLK + j)
            expert_pair(E // 2 - 1, last=True)

        @block.tensor
        def _(pe):
            def transposes(c):
                for q in range(2 * c, 2 * c + 2):
                    if q >= 2:
                        pe.wait_ge(lo_done, q - 1)
                    for t in range(2):
                        pe.wait_ge(xn_done, 2 * q + t + 1)
                        for k in range(KC):
                            at = 2 * P * k + P * t
                            last = pe.transpose(banks[q % 2][:, at:at + P], xn[:, (2 * q + t) % TB, P * k:P * (k + 1)], ident[:, :])
                    last.then_inc(tp_done, 1)

            def xT(k, sl):
                return xT_hi[:, k, sl], xT_lo[:, k, sl]

            def maximum_product(m, p, v, bank):
                head, qt = v // KT, v % KT
                for half in range(2):
                    last = pe.matmul(banks[bank + half], QS[p][0:KROWS, head, P * qt:P * (qt + 1)],
                                     KS[p][0:KROWS, BANK * half:BANK * (half + 1)], start=True, stop=True)
                last.then_inc(mx_done, 1)

            early = iter(range(N_EARLY))

            def early_pair(c, i):
                if i >= EARLY.get(c, 0):
                    return
                v = next(early)
                if v == 0:
                    pe.wait_ge(stacks_loaded[0], 16 * 2 * NPART)
                elif i == 0:
                    pe.wait_ge(mx_read, v)
                elif i == 1:
                    pe.wait_ge(lo_done, 2 * c + 4)
                else:
                    pe.wait_ge(mx_read, v - 1)
                maximum_product(0, 0, v, EARLY_BANKS[i])

            def project(c):
                sl = slice(BANK * c, BANK * (c + 1))
                pe.wait_ge(lo_done, 2 * c + 2)
                if c == 0:
                    pe.wait_ge(wa_lo_done, 1)
                for j in range(3):
                    if c >= 1:
                        pe.wait_ge(rest_done, 3 * (c - 1) + j + 1)
                    M = P if j < 2 else KV
                    lhs = [(wa_hi[:, k, P * j:P * j + M], wa_lo[:, k, P * j:P * j + M]) for k in range(KC)]
                    three(pe, banks[2 + j][0:M, :], lhs, [xT(k, sl) for k in range(KC)]).then_inc(qk_done, 1)

            def project_by_token(c):
                if c >= 1:
                    pe.wait_ge(vr_read, 2 * c)
                for t in range(TB):
                    at = BANK * c + P * t
                    rhs = [(wa_hi[:, k, D + KV:WA], wa_lo[:, k, D + KV:WA]) for k in range(KC)]
                    last = three(pe, banks[5][:, VR * t:VR * (t + 1)], [xT(k, slice(at, at + P)) for k in range(KC)], rhs)
                last.then_inc(vr_done, 1)

            pe.wait_ge(consts, 5)
            transposes(0)
            for c in range(NBLK):
                project(c)
                if c + 1 < NBLK:
                    if c in EARLY and c - 1 in EARLY:
                        pe.wait_ge(mx_read, sum(EARLY.get(b, 0) for b in range(c - 1)) + 2)
                    transposes(c + 1)
                early_pair(c, 0)
                project_by_token(c)
                early_pair(c, 1)
                early_pair(c, 2)

            def max_pair(m, p, v):
                pe.wait_ge(mx_read, PAIRS * m + v - 1)
                if v == 1:
                    pe.wait_ge(mrows_done, m)
                maximum_product(m, p, v, pair_bank(v))

            def turn_maxima(m):
                pe.wait_ge(mparts_done, m + 1)
                pe.transpose(banks[3][0:3 * PAIRS, 0:P // 2].bitcast(BF16),
                             mparts[:, :, :].rearrange("p a q -> p (a q)"), ident_bf[:, :]).then_inc(mT_done, 1)

            def values(n, i, p, s):
                kt = s % KT
                pe.wait_ge(exp_done, UNITS * n + REP * (s + 1) + EXP0)
                if kt == 0:
                    pe.wait_ge(o_done, 2 * n + s // KT + O0)
                if s == 0:
                    pe.wait_ge(v_loaded[p], 16 * i + 32)
                for r in range(REP):
                    last = pe.matmul(banks[7][2 * HD * r:2 * HD * (r + 1), :], V[p][:, kt, :], probs[s % 2][:, r, :],
                                     start=(kt == 0), stop=(kt == KT - 1))
                last.then_inc(pv_done, 1)

            def beside(n, i, p, s, k, more):
                begin, end = slot(s, k)
                if more >= 1:
                    for v, at in enumerate(places(PASS, PAIRS - AHEAD)):
                        if begin < at <= end:
                            max_pair(n + 1, (p + 1) % RING, AHEAD + v)
                    if begin < TURN_AT <= end:
                        turn_maxima(n + 1)
                if more >= 2:
                    for v, at in enumerate(places(NEXT_PASS, AHEAD)):
                        if begin < at <= end:
                            if v == 0:
                                pe.wait_ge(stacks_loaded[(p + 2) % RING], 16 * 2 * NPART * (i + (p + 2) // RING + 1))
                            max_pair(n + 2, (p + 2) % RING, v)

            def attend(n, i, p, more=2):
                pe.wait_ge(negmax_loaded, 16 * n + 16)
                if more == 0:
                    pe.wait_ge(mx_read, PAIRS * NGRP)
                    pe.wait_ge(mrows_done, NGRP)
                for s in range(STEPS):
                    qb, kt = s // KT, s % KT
                    for r in range(REP):
                        u = REP * s + r
                        if more or u < 3:
                            pe.wait_ge(exp_done, UNITS * n + u - 2 + EXP0)
                        elif u >= 7:
                            pe.wait_ge(exp_done, UNITS * n + u - 6 + EXP0)
                        pe.matmul(banks[bank_of(u, p, not more)], KS[p][0:KROWS + 3, P * kt:P * (kt + 1)],
                                  QS[p][0:KROWS + 3, r, BANK * qb:BANK * (qb + 1)], start=True, stop=True).then_inc(st_done, 1)
                        beside(n, i, p, s, r, more)
                        if r == 2:
                            if s > 0:
                                values(n, i, p, s - 1)
                            elif not isinstance(n, int) or n > 0:
                                values(n - 1, None, (p - 1) % RING, STEPS - 1)

            pe.wait_ge(rest_done, 3 * NBLK)
            pe.wait_ge(vr_read, 2 * NBLK)
            pe.wait_ge(mx_read, N_EARLY)
            for v in range(N_EARLY, PAIRS):
                max_pair(0, 0, v)
            turn_maxima(0)
            pe.wait_ge(stacks_loaded[1], 16 * 2 * NPART)
            for v in range(AHEAD):
                max_pair(1, 1, v)
            attend(0, 0, 0)
            with pe.Fori(0, NGRP // RING - 1) as i:
                for p in range(RING):
                    attend(RING * i + p + 1, i + (p + 1) // RING, (p + 1) % RING)
            for n in range(NGRP // RING * RING - RING + 1, NGRP):
                attend(n, n // RING, n % RING, min(2, NGRP - 1 - n))
            values(NGRP - 1, None, (NGRP - 1) % RING, STEPS - 1)

            def project_attn(n):
                if n == 0:
                    pe.wait_ge(wa_lo_done, 2)
                pe.wait_ge(alo_done, n + 1)
                r = turn(2 * n + 1) + 1
                for t in range(TB):
                    if r >= 2 and t % 2 == 0:
                        pe.wait_ge(acc_done, TB * (r - 2) + t + 2)
                    lhs = [(attn_hi[:, k, P * t:P * (t + 1)], attn_lo[:, k, P * t:P * (t + 1)]) for k in range(KC)]
                    rhs = [(wo_hi[:, k, :], wo_lo[:, k, :]) for k in range(KC)]
                    last = three(pe, banks[4 + 2 * (r % 2) + t // 2][:, D * (t % 2):D * (t % 2 + 1)], lhs, rhs)
                    if t % 2:
                        last.then_inc(y_done, 1)

            def gate_up(k, blk, p, par, first=False):
                sl = slice(BANK * blk, BANK * (blk + 1))
                rhs = [xT(c, sl) for c in range(KC)]
                for m, (read, done) in enumerate(((silu_done, g_done), (h_done, u_done))):
                    if not first:
                        pe.wait_ge(read, k - 1)
                    at = KC * I * m
                    lhs = [(w_hi[p][:, at + I * c:at + I * (c + 1)], w_lo[p][:, at + I * c:at + I * (c + 1)]) for c in range(KC)]
                    three(pe, banks[2 * m + par][:, :], lhs, rhs).then_inc(done, 1)

            def down(k, j, p):
                pe.wait_ge(hlo_done, k + 1)
                r = turn(k)
                for t in range(TB):
                    if t % 2 == 0 and not (isinstance(r, int) and r < 2):
                        pe.wait_ge(acc_done, TB * r - 2 * TB + t + 2)
                    sl = slice(P * t, P * (t + 1))
                    at = 2 * KC * I
                    par = r % 2 if isinstance(r, int) else j % 2
                    last = three(pe, banks[4 + 2 * par + t // 2][:, D * (t % 2):D * (t % 2 + 1)],
                                 [(h_hi[j % 2][:, sl], h_lo[j % 2][:, sl])], [(w_hi[p][:, at:WE], w_lo[p][:, at:WE])])
                    if t % 2:
                        last.then_inc(y_done, 1)

            pe.wait_ge(wlo_done, 1)
            gate_up(0, 0, 0, 0, True)
            pe.wait_ge(o_done, 2 * NGRP + O0)

            def expert_pair(i, last=False, first=False):
                for p in range(2):
                    for j in range(NBLK):
                        k = 2 * NBLK * i + NBLK * p + j
                        final = last and p == 1
                        if not (final and j == NBLK - 1):
                            if j == NBLK - 1:
                                pe.wait_ge(wlo_done, 2 * i + p + 2)
                                gate_up(k + 1, 0, 1 - p, 0)
                            else:
                                gate_up(k + 1, j + 1, p, (j + 1) % 2, first and k == 0)
                        down(k, j, p)
                        if first and j % 2 == 1:
                            project_attn(k // 2)

            expert_pair(0, first=True)
            with pe.Fori(1, E // 2 - 1) as i:
                expert_pair(i)
            expert_pair(E // 2 - 1, last=True)


def kernel(L0_attn_x, L0_attn_Wq, L0_attn_Wk, L0_attn_Wv, L0_attn_Wo, L0_ffn_router_weight, L0_ffn_router_bias,
           L0_ffn_w_gate, L0_ffn_w_up, L0_ffn_w_down):
    import numpy as np
    import concourse.bacc as bacc
    from concourse.bass_utils import run_bass_kernel_spmd

    head_dim, D = 16, L0_attn_Wo.shape[1]
    wo_rows = np.transpose(np.reshape(L0_attn_Wo, (-1, head_dim, D)), (1, 0, 2))
    arrays = {
        "x_in": L0_attn_x, "wq_in": L0_attn_Wq, "wk_in": L0_attn_Wk, "wv_in": L0_attn_Wv, "wo_in": wo_rows,
        "wr_in": np.transpose(L0_ffn_router_weight), "bias_in": L0_ffn_router_bias,
        "wg_in": np.transpose(L0_ffn_w_gate, (0, 2, 1)), "wu_in": np.transpose(L0_ffn_w_up, (0, 2, 1)),
        "wd_in": np.transpose(L0_ffn_w_down, (0, 2, 1)),
    }
    arrays = {name: np.ascontiguousarray(a) for name, a in arrays.items()}
    nc = bacc.Bacc("TRN2", target_bir_lowering=False, num_devices=1)
    ins = [nc.dram_tensor(name, a.shape, mybir.dt.from_np(a.dtype), kind="ExternalInput").ap() for name, a in arrays.items()]
    out = nc.dram_tensor("out", arrays["x_in"].shape, F32, kind="ExternalOutput").ap()
    build_layer(nc, *ins, out)
    result = run_bass_kernel_spmd(nc, [arrays], core_ids=[0])
    return result.results[0]["out"]
```
